# Optimizing a Trainium2 kernel written in Bass

```python
import numpy as np
import jax
import jax.numpy as jnp

def _softmax(x, axis=-1):
    return jax.nn.softmax(x, axis=axis)
def _gelu(x):
    return jax.nn.gelu(x, approximate=True)
def _silu(x):
    return jax.nn.silu(x)
def _sigmoid(x):
    return jax.nn.sigmoid(x)
def _layernorm(x, axis=-1, eps=1e-5):
    m = jnp.mean(x, axis=axis, keepdims=True)
    v = jnp.var(x, axis=axis, keepdims=True)
    return (x - m) / jnp.sqrt(v + eps)
def _scatter_add(tgt, idx, src, axis=0):
    return tgt.at[idx].add(src)
def _segment_sum(src, seg, n):
    return jax.ops.segment_sum(src, seg, n)

kernel_name = 'mk_conv_preact_d1_conv_nchw64_f793cb'

def setup_inputs(seed: int = 0):
    np.random.seed(seed)
    _w = jnp.asarray
    def _rec_inputs():
        import jax
        import jax.numpy as jnp
        _gk = jax.random.key(seed)
        x = -0.0002091 + 1 * jax.random.normal(jax.random.fold_in(_gk, 1), (8, 64, 224, 224), jnp.float32)
        return x
    x = _rec_inputs()
    def _L0_conv_setup():
        import jax, jax.numpy as jnp
        import numpy as np
        B, C, H, W = (8, 64, 224, 224)
        C3 = 3 * C
        DEC_LO = [-0.07576571478927333, -0.02963552764599851, 0.49761866763201545, 0.8037387518059161, 0.29785779560527736, -0.09921954357684722, -0.012603967262037833, 0.0322231006040427]
        DEC_HI = [-0.0322231006040427, -0.012603967262037833, 0.09921954357684722, 0.29785779560527736, -0.8037387518059161, 0.49761866763201545, 0.02963552764599851, -0.07576571478927333]
        _MX = [0, 0, 6, 0, 0, 1, 1, 4, 5, 1, 3, 0, 0, 0, 3, 2]
        _MY = [0, 1, 0, 5, 2, 0, 2, 0, 0, 6, 0, 4, 6, 3, 5, 2]
        _S = H // 7

        def _dct_filter(h, w, mapper_x, mapper_y, channel):
            cp = channel // len(mapper_x)

            def basis(u, n):
                b = np.cos(np.pi * u * (np.arange(n) + 0.5) / n) / np.sqrt(n)
                return b * np.sqrt(2.0) if u != 0 else b
            filt = np.zeros((channel, h, w), np.float32)
            for i, (u, v) in enumerate(zip(mapper_x, mapper_y)):
                filt[i * cp:(i + 1) * cp] = np.outer(basis(u, h), basis(v, w))
            return jnp.asarray(filt)
        DCT_LOW = _dct_filter(H, W, [u * _S for u in _MX], [v * _S for v in _MY], C)
        DCT_HIGH = _dct_filter(H, W, [u * _S for u in _MX], [v * _S for v in _MY], C3)

        def _circ(x, filt, dil, axis):
            return sum((fk * jnp.roll(x, -k * dil, axis=axis) for k, fk in enumerate(filt)))

        def _swt2_level3(a):
            for dil in (1, 2):
                a = _circ(_circ(a, DEC_LO, dil, 1), DEC_LO, dil, 2)
            d = 4
            aL = _circ(a, DEC_LO, d, 1)
            aH = _circ(a, DEC_HI, d, 1)
            cA = _circ(aL, DEC_LO, d, 2)
            cH = _circ(aL, DEC_HI, d, 2)
            cV = _circ(aH, DEC_LO, d, 2)
            cD = _circ(aH, DEC_HI, d, 2)
            return (cA, cH, cV, cD)

        def conv3x3(x, w, b):
            y = jax.lax.conv_general_dilated(x, w, (1, 1), ((1, 1), (1, 1)), dimension_numbers=('NCHW', 'OIHW', 'NCHW'))
            return y + b[None, :, None, None]

        def conv1x1(x, w, b):
            return jnp.einsum('oc,nchw->nohw', w, x) + b[None, :, None, None]

        def _attention(x, dctw, Wd, bd, Wa, ba, W1, W2):
            y = jnp.sum(conv1x1(x, Wd, bd) * dctw[None], axis=(2, 3))
            scale = jax.nn.sigmoid(jax.nn.relu(y @ W1.T) @ W2.T)
            return conv1x1(x, Wa, ba) * scale[:, :, None, None]
        key = jax.random.key(seed)
        ks = jax.random.split(key, 17)

        def nrm(k, shape, scale=1.0):
            return (jax.random.normal(k, shape) * scale).astype(jnp.float32)
        return {'x': nrm(ks[0], (B, C, H, W)), 'W_id': nrm(ks[1], (C, C, 3, 3), 1 / np.sqrt(C * 9)), 'b_id': nrm(ks[2], (C,), 0.01), 'W_dl': nrm(ks[3], (C, C), 1 / np.sqrt(C)), 'b_dl': nrm(ks[4], (C,), 0.01), 'W_al': nrm(ks[5], (C, C), 1 / np.sqrt(C)), 'b_al': nrm(ks[6], (C,), 0.01), 'W1_low': nrm(ks[7], (C // 16, C), 1 / np.sqrt(C)), 'W2_low': nrm(ks[8], (C, C // 16), 1 / np.sqrt(C // 16)), 'W_dh': nrm(ks[9], (C3, C3), 1 / np.sqrt(C3)), 'b_dh': nrm(ks[10], (C3,), 0.01), 'W_ah': nrm(ks[11], (C3, C3), 1 / np.sqrt(C3)), 'b_ah': nrm(ks[12], (C3,), 0.01), 'W1_high': nrm(ks[13], (C3 // 16, C3), 1 / np.sqrt(C3)), 'W2_high': nrm(ks[14], (C3, C3 // 16), 1 / np.sqrt(C3 // 16)), 'W_enc': nrm(ks[15], (C, 4 * C, 3, 3), 1 / np.sqrt(4 * C * 9)), 'b_enc': nrm(ks[16], (C,), 0.01)}
    _L0_conv_all = _L0_conv_setup()
    _L0_conv_in = {k: v for k, v in _L0_conv_all.items() if k in ('W_id', 'b_id', 'W_dl', 'b_dl', 'W_al', 'b_al', 'W1_low', 'W2_low', 'W_dh', 'b_dh', 'W_ah', 'b_ah', 'W1_high', 'W2_high', 'W_enc', 'b_enc', )}
    del _L0_conv_all

    return {
        "x": x,
        "L0_conv_W_id": _L0_conv_in["W_id"],
        "L0_conv_b_id": _L0_conv_in["b_id"],
        "L0_conv_W_dl": _L0_conv_in["W_dl"],
        "L0_conv_b_dl": _L0_conv_in["b_dl"],
        "L0_conv_W_al": _L0_conv_in["W_al"],
        "L0_conv_b_al": _L0_conv_in["b_al"],
        "L0_conv_W1_low": _L0_conv_in["W1_low"],
        "L0_conv_W2_low": _L0_conv_in["W2_low"],
        "L0_conv_W_dh": _L0_conv_in["W_dh"],
        "L0_conv_b_dh": _L0_conv_in["b_dh"],
        "L0_conv_W_ah": _L0_conv_in["W_ah"],
        "L0_conv_b_ah": _L0_conv_in["b_ah"],
        "L0_conv_W1_high": _L0_conv_in["W1_high"],
        "L0_conv_W2_high": _L0_conv_in["W2_high"],
        "L0_conv_W_enc": _L0_conv_in["W_enc"],
        "L0_conv_b_enc": _L0_conv_in["b_enc"],
    }

def reference(x, L0_conv_W_id, L0_conv_b_id, L0_conv_W_dl, L0_conv_b_dl, L0_conv_W_al, L0_conv_b_al, L0_conv_W1_low, L0_conv_W2_low, L0_conv_W_dh, L0_conv_b_dh, L0_conv_W_ah, L0_conv_b_ah, L0_conv_W1_high, L0_conv_W2_high, L0_conv_W_enc, L0_conv_b_enc):
    import jax
    import jax.numpy as jnp
    def _L0_conv_ref(x, W_id, b_id, W_dl, b_dl, W_al, b_al, W1_low, W2_low, W_dh, b_dh, W_ah, b_ah, W1_high, W2_high, W_enc, b_enc):
        import jax, jax.numpy as jnp
        import numpy as np
        B, C, H, W = (8, 64, 224, 224)
        C3 = 3 * C
        DEC_LO = [-0.07576571478927333, -0.02963552764599851, 0.49761866763201545, 0.8037387518059161, 0.29785779560527736, -0.09921954357684722, -0.012603967262037833, 0.0322231006040427]
        DEC_HI = [-0.0322231006040427, -0.012603967262037833, 0.09921954357684722, 0.29785779560527736, -0.8037387518059161, 0.49761866763201545, 0.02963552764599851, -0.07576571478927333]
        _MX = [0, 0, 6, 0, 0, 1, 1, 4, 5, 1, 3, 0, 0, 0, 3, 2]
        _MY = [0, 1, 0, 5, 2, 0, 2, 0, 0, 6, 0, 4, 6, 3, 5, 2]
        _S = H // 7

        def _dct_filter(h, w, mapper_x, mapper_y, channel):
            cp = channel // len(mapper_x)

            def basis(u, n):
                b = np.cos(np.pi * u * (np.arange(n) + 0.5) / n) / np.sqrt(n)
                return b * np.sqrt(2.0) if u != 0 else b
            filt = np.zeros((channel, h, w), np.float32)
            for i, (u, v) in enumerate(zip(mapper_x, mapper_y)):
                filt[i * cp:(i + 1) * cp] = np.outer(basis(u, h), basis(v, w))
            return jnp.asarray(filt)
        DCT_LOW = _dct_filter(H, W, [u * _S for u in _MX], [v * _S for v in _MY], C)
        DCT_HIGH = _dct_filter(H, W, [u * _S for u in _MX], [v * _S for v in _MY], C3)

        def _circ(x, filt, dil, axis):
            return sum((fk * jnp.roll(x, -k * dil, axis=axis) for k, fk in enumerate(filt)))

        def _swt2_level3(a):
            for dil in (1, 2):
                a = _circ(_circ(a, DEC_LO, dil, 1), DEC_LO, dil, 2)
            d = 4
            aL = _circ(a, DEC_LO, d, 1)
            aH = _circ(a, DEC_HI, d, 1)
            cA = _circ(aL, DEC_LO, d, 2)
            cH = _circ(aL, DEC_HI, d, 2)
            cV = _circ(aH, DEC_LO, d, 2)
            cD = _circ(aH, DEC_HI, d, 2)
            return (cA, cH, cV, cD)

        def conv3x3(x, w, b):
            y = jax.lax.conv_general_dilated(x, w, (1, 1), ((1, 1), (1, 1)), dimension_numbers=('NCHW', 'OIHW', 'NCHW'))
            return y + b[None, :, None, None]

        def conv1x1(x, w, b):
            return jnp.einsum('oc,nchw->nohw', w, x) + b[None, :, None, None]

        def _attention(x, dctw, Wd, bd, Wa, ba, W1, W2):
            y = jnp.sum(conv1x1(x, Wd, bd) * dctw[None], axis=(2, 3))
            scale = jax.nn.sigmoid(jax.nn.relu(y @ W1.T) @ W2.T)
            return conv1x1(x, Wa, ba) * scale[:, :, None, None]
        res = conv3x3(x, W_id, b_id)
        cA, cH, cV, cD = _swt2_level3(x[0])
        cA_t = cA[None]
        high = jnp.stack([cH, cV, cD], axis=1).reshape(1, C3, H, W)
        low_att = _attention(cA_t, DCT_LOW, W_dl, b_dl, W_al, b_al, W1_low, W2_low)
        high_att = _attention(high, DCT_HIGH, W_dh, b_dh, W_ah, b_ah, W1_high, W2_high)
        dmt = jnp.concatenate([low_att, high_att], axis=1)
        out = jax.nn.leaky_relu(conv3x3(dmt, W_enc, b_enc), 0.01)
        return out + res

    def _gn(v, G=32, eps=1e-5):
        B_, C_, H_, W_ = v.shape
        g = v.reshape(B_, G, C_ // G, H_, W_)
        m = jnp.mean(g, axis=(2, 3, 4), keepdims=True)
        s = jnp.var(g, axis=(2, 3, 4), keepdims=True)
        return ((g - m) / jnp.sqrt(s + eps)).reshape(v.shape)

    def _ln_c(v, eps=1e-6):
        m = jnp.mean(v, axis=1, keepdims=True)
        s = jnp.var(v, axis=1, keepdims=True)
        return (v - m) / jnp.sqrt(s + eps)

    def _ln_t(v, eps=1e-5):
        m = jnp.mean(v, axis=-1, keepdims=True)
        s = jnp.var(v, axis=-1, keepdims=True)
        return (v - m) / jnp.sqrt(s + eps)

    def _to_tokens(v):
        B_, C_, H_, W_ = v.shape
        return v.reshape(B_, C_, H_ * W_).transpose(0, 2, 1)
    def _from_tokens(t, like):
        B_, C_, H_, W_ = like.shape
        return t.transpose(0, 2, 1).reshape(B_, C_, H_, W_)

    x = x + _L0_conv_ref(_gn(x), L0_conv_W_id, L0_conv_b_id, L0_conv_W_dl, L0_conv_b_dl, L0_conv_W_al, L0_conv_b_al, L0_conv_W1_low, L0_conv_W2_low, L0_conv_W_dh, L0_conv_b_dh, L0_conv_W_ah, L0_conv_b_ah, L0_conv_W1_high, L0_conv_W2_high, L0_conv_W_enc, L0_conv_b_enc)
    return x


_drawn_inputs = setup_inputs


def setup_inputs(seed=0):
    import zlib

    import numpy as np

    out = dict(_drawn_inputs(seed))
    spreads = {}
    factors = {'L0_conv_b_id': 8.0,
     'L0_conv_b_dl': 5.556,
     'L0_conv_b_al': 29.269,
     'L0_conv_b_ah': 27.209,
     'L0_conv_b_enc': 8.0}
    for name, (base, spread) in spreads.items():
        noise = np.random.default_rng([zlib.crc32(name.encode()), seed]).standard_normal(out[name].shape)
        drawn = base * np.exp(spread * noise) if base else spread * noise
        out[name] = jnp.asarray(drawn.astype(out[name].dtype))
    for name, factor in factors.items():
        out[name] = (out[name] * factor).astype(out[name].dtype)
    return out
```

```python
from contextlib import ExitStack

import numpy as np

import concourse.bass as bass
from concourse import mybir

ALU = mybir.AluOpType
ACT = mybir.ActivationFunctionType
AX = mybir.AxisListType
F32 = mybir.dt.float32
F16 = mybir.dt.float16

B, C, H, W = 8, 64, 224, 224
HW = H * W
G = 32
P = 128
HALF = H // 2
EPS = 1e-5
TAPS = 9
WP = W + 2

R = 8
NB = HALF // R
RH = R + 2
PAIRS = R // 2
NT = 2 * W
XS = 4
INNER = 3

SR_EDGE = 2
SR_IN = 6
SC = SR_IN * W
NSTAT = HALF // 2

ER = 4
NE = HALF // ER
EH = ER + 2
SROWS = H + 2 + ER
CG = 8

DEC_LO = [-0.07576571478927333, -0.02963552764599851, 0.49761866763201545, 0.8037387518059161,
          0.29785779560527736, -0.09921954357684722, -0.012603967262037833, 0.0322231006040427]
DEC_HI = [-0.0322231006040427, -0.012603967262037833, 0.09921954357684722, 0.29785779560527736,
          -0.8037387518059161, 0.49761866763201545, 0.02963552764599851, -0.07576571478927333]
MX = [0, 0, 6, 0, 0, 1, 1, 4, 5, 1, 3, 0, 0, 0, 3, 2]
MY = [0, 1, 0, 5, 2, 0, 2, 0, 0, 6, 0, 4, 6, 3, 5, 2]
NK = len(MX)
NF = 7
SUM_L = float(np.sum(DEC_LO) ** 3)
SUM_H = float(np.sum(DEC_LO) ** 2 * np.sum(DEC_HI))
NG = 2 * NF
NS1 = 2 * H + NG
SUBBAND = [1, 2, 3]


def constants():
    def circulant(taps, dil):
        m = np.zeros((H, H))
        for k, f in enumerate(taps):
            for i in range(H):
                m[i, (i + k * dil) % H] += f
        return m

    level2 = circulant(DEC_LO, 2) @ circulant(DEC_LO, 1)
    low, high = circulant(DEC_LO, 4) @ level2, circulant(DEC_HI, 4) @ level2
    basis = np.zeros((NF, H))
    for u in range(NF):
        f = u * (H // 7)
        basis[u] = np.cos(np.pi * f * (np.arange(H) + 0.5) / H) / np.sqrt(H) * (np.sqrt(2.0) if f else 1.0)
    moved = np.concatenate([low.T @ basis.T, high.T @ basis.T], axis=1)
    fh = np.concatenate([low.T, high.T, moved], axis=1)
    fw = np.concatenate([low.T, high.T], axis=1)
    fw_hi = fw.astype(np.float16)
    fw_lo = (fw - fw_hi.astype(np.float64)).astype(np.float16)
    total = moved.sum(axis=0)
    of_mean = np.outer(total, total).reshape(1, NG * NG).repeat(C, axis=0)
    partner = np.zeros((P, 3, P))
    for p in range(P):
        for k, q in enumerate((p ^ 1, p ^ C, p ^ 1 ^ C)):
            partner[q, k, p] = 1.0
    pick = np.zeros((96, 3, NK))
    dsum = np.zeros((96, 3))
    bsum = basis.sum(axis=1)
    for g in range(3):
        for o in range(C if g == 0 else 96):
            k = o // (C // NK) if g == 0 else (96 * (g - 1) + o) // (3 * C // NK)
            pick[o, g, k] = 1.0
            dsum[o, g] = bsum[MX[k]] * bsum[MY[k]]
    inside = np.zeros((TAPS, H + ER, W), np.float16)
    for t in range(TAPS):
        dy, dx = t // 3 - 1, t % 3 - 1
        inside[t, max(0, -dy):H - max(0, dy), max(0, -dx):W - max(0, dx)] = 1.0
    f = np.float32
    return {
        "fh": fh.reshape(2, HALF, NS1).transpose(1, 0, 2).astype(f),
        "fw": np.stack([fw_hi, fw_lo], 1).reshape(2, HALF, 2, 2 * W).transpose(1, 0, 2, 3),
        "gw": moved.reshape(2, HALF, NG).transpose(1, 0, 2).astype(f),
        "of_mean": of_mean.astype(f),
        "partner": partner.astype(f),
        "ident": np.eye(C, dtype=f),
        "pick": pick.astype(f),
        "dsum": dsum.astype(f),
        "inside": inside.reshape(TAPS, (H + ER) * W),
    }


def conv_preact(nc, t, out):
    x = t["x"]
    scratch = nc.dram_tensor("row_filtered", (2, HALF, SROWS, 2 * P), F16, kind="Internal").ap()

    with ExitStack() as top:
        def sb(stack, name, shape, dt=F32):
            return stack.enter_context(nc.sbuf_tensor(name, shape, dt))

        def sem(stack, name):
            return stack.enter_context(nc.semaphore(name))

        psum = [top.enter_context(nc.psum_tensor(f"ps{i}", [P, 512], F32)) for i in range(8)]
        partner = sb(top, "partner", [P, 3, P])
        records = sb(top, "records", [P, NSTAT, 6])
        mv = sb(top, "mv", [P, 2])
        quad = sb(top, "quad", [P, 4, 2])
        gsum = sb(top, "gsum", [P, 2])
        gmean = sb(top, "gmean", [P, 1])
        dev = sb(top, "dev", [P, 4])
        dev2 = sb(top, "dev2", [P, 4])
        gvar = sb(top, "gvar", [P, 1])
        mhalf = sb(top, "mhalf", [P, 1])
        root = sb(top, "root", [P, 1])
        newt = sb(top, "newt", [P, 2])
        norm = sb(top, "norm", [P, 2])
        w_hi = sb(top, "w_hi", [P, TAPS, C], F16)
        w_lo = [sb(top, f"w_lo{s}", [P, 6, C], F16) for s in range(2)]
        w_max = sb(top, "w_max", [P, 1])
        b_id = sb(top, "b_id", [P, 1])

        def combine(dve, chain, base, ps):
            def step(n, ins):
                ins.then_inc(chain, 1)
                dve.wait_ge(chain, base + n)
            step(1, dve.tensor_copy(quad[:, 1:4, :], ps))
            step(2, dve.tensor_copy(quad[:, 0, :], mv[:, :]))
            step(3, dve.tensor_reduce(gsum[:, 0:1], quad[:, :, 0], AX.X, ALU.add))
            step(4, dve.tensor_scalar(gmean[:, :], gsum[:, 0:1], 0.25, None, ALU.mult))
            step(5, dve.tensor_scalar(dev[:, :], quad[:, :, 0], gmean[:, 0:1], None, ALU.subtract))
            step(6, dve.tensor_tensor(dev2[:, :], dev[:, :], dev[:, :], ALU.mult))
            step(7, dve.tensor_tensor(dev[:, :], dev2[:, :], quad[:, :, 1], ALU.add))
            step(8, dve.tensor_reduce(gsum[:, 1:2], dev[:, :], AX.X, ALU.add))

        def commit(dve, chain, base):
            def step(n, ins):
                ins.then_inc(chain, 1)
                dve.wait_ge(chain, base + n)
            step(1, dve.tensor_tensor(newt[:, 0:1], root[:, :], root[:, :], ALU.mult))
            step(2, dve.tensor_tensor(newt[:, 1:2], newt[:, 0:1], gvar[:, :], ALU.mult))
            step(3, dve.tensor_scalar(newt[:, 0:1], newt[:, 1:2], -0.5, 1.5, ALU.mult, ALU.add))
            step(4, dve.tensor_tensor(norm[:, 0:1], root[:, :], newt[:, 0:1], ALU.mult))
            step(5, dve.scalar_tensor_tensor(norm[:, 1:2], gmean[:, :], -1.0, norm[:, 0:1],
                                             ALU.mult, ALU.mult))

        with ExitStack() as s1:
            CR = 14
            NCH = HALF // CR
            xc = [sb(s1, f"xc{i}", [P, CR * W]) for i in range(2)]
            w32 = sb(s1, "w32", [P, TAPS, C])
            wn = sb(s1, "wn", [P, TAPS, C])
            wl = sb(s1, "wl", [P, TAPS, C], F16)
            wmx = sb(s1, "wmx", [P, 2])
            winv = sb(s1, "winv", [P, 1])
            chunk_in = [sem(s1, f"chunk_in{i}") for i in range(2)]
            consts_in = sem(s1, "consts_in")
            chunk_used = sem(s1, "chunk_used")
            aggregated = sem(s1, "aggregated")
            partners_done = sem(s1, "partners_done")
            chain1 = sem(s1, "chain1")
            mhalf_set = sem(s1, "mhalf_set")
            var_ready = sem(s1, "var_ready")
            root_ready = sem(s1, "root_ready")
            wmax_part = sem(s1, "wmax_part")
            wmax_all = sem(s1, "wmax_all")
            wchain = sem(s1, "wchain")

            with nc.Block() as block:
                @block.sync
                def _(sp):
                    sp.dma_start(partner[:, :, :], t["partner"]).then_inc(consts_in, 16)
                    for s in range(2):
                        sp.dma_start(w32[C * s:C * s + C, :, :], t["w_id"]).then_inc(consts_in, 16)
                        sp.dma_start(b_id[C * s:C * s + C, :], t["b_id"]).then_inc(consts_in, 16)
                    with sp.Fori(0, NCH // 2) as i:
                        for n in range(2):
                            sp.wait_ge(chunk_used, 2 * i + n + 1)
                            for s in range(2):
                                src = x[0, :, bass.ds(s * HALF + (2 * i + n) * CR, CR), :]
                                sp.dma_start(xc[n][C * s:C * s + C, :],
                                             src.rearrange("c h w -> c (h w)")).then_inc(chunk_in[n], 16)

                @block.vector
                def _(dve):
                    def step(n, ins):
                        ins.then_inc(wchain, 1)
                        dve.wait_ge(wchain, n)
                    dve.memset(mhalf[:, :], -0.5).then_inc(mhalf_set, 1)
                    dve.memset(winv[:, :], 0.0).then_inc(chunk_used, 2)
                    dve.wait_ge(chunk_used, 2)
                    for s in range(2):
                        dve.memset(w_lo[s][:, :, :], 0.0).then_inc(mhalf_set, 1)
                    dve.wait_ge(mhalf_set, 3)
                    dve.wait_ge(consts_in, 80)
                    dve.tensor_reduce(wmx[:, 0:1], w32[:, :, :].rearrange("p a b -> p (a b)"), AX.X, ALU.max,
                                      apply_absolute_value=True).then_inc(wmax_part, 1)
                    dve.wait_ge(wmax_all, 1)
                    step(1, dve.tensor_scalar(w_max[:, :], wmx[:, 1:2], 1e-30, None, ALU.max))
                    step(2, dve.reciprocal(winv[:, :], w_max[:, :]))
                    step(3, dve.tensor_scalar(wn[:, :, :], w32[:, :, :], winv[:, 0:1], None, ALU.mult))
                    step(4, dve.tensor_copy(w_hi[:, :, :], wn[:, :, :]))
                    step(5, dve.tensor_tensor(wl[:, :, :], wn[:, :, :], w_hi[:, :, :], ALU.subtract))
                    own, other = slice(0, 3), slice(3, 6)
                    step(6, dve.tensor_copy(w_lo[0][0:C, 0:3, :], wl[0:C, own, :]))
                    step(7, dve.tensor_copy(w_lo[0][C:P, 0:3, :], wl[C:P, other, :]))
                    step(8, dve.tensor_copy(w_lo[0][C:P, 3:6, :], wl[C:P, 6:9, :]))
                    step(9, dve.tensor_copy(w_lo[1][C:P, 0:3, :], wl[C:P, own, :]))
                    step(10, dve.tensor_copy(w_lo[1][0:C, 0:3, :], wl[0:C, other, :]))
                    step(11, dve.tensor_copy(w_lo[1][0:C, 3:6, :], wl[0:C, 6:9, :]))
                    per = CR // 2
                    with dve.Fori(0, NCH // 2) as i:
                        for n in range(2):
                            dve.wait_ge(chunk_in[n], 32 * i + 32)
                            for k in range(per):
                                ins = dve.bn_stats(
                                    records[:, bass.ds((2 * i + n) * per + k, 1), :].rearrange("p a b -> p (a b)"),
                                    xc[n][:, k * NT:k * NT + NT])
                            ins.then_inc(chunk_used, 1)
                    dve.wait_ge(chunk_used, NCH + 2)
                    dve.bn_aggr(mv[:, :], records[:, :, :].rearrange("p a b -> p (a b)")).then_inc(aggregated, 1)
                    dve.wait_ge(partners_done, 1)
                    combine(dve, chain1, 0, psum[7][:, 0:6].rearrange("p (a b) -> p a b", a=3))
                    dve.tensor_scalar(gvar[:, :], gsum[:, 1:2], 0.25, EPS, ALU.mult, ALU.add).then_inc(var_ready, 1)
                    dve.wait_ge(root_ready, 1)
                    commit(dve, chain1, 8)

                @block.tensor
                def _(pe):
                    pe.wait_ge(consts_in, 80)
                    pe.wait_ge(aggregated, 1)
                    for k in range(3):
                        mm = pe.matmul(psum[7][:, 2 * k:2 * k + 2], partner[:, k, :], mv[:, :], start=True, stop=True)
                    mm.then_inc(partners_done, 1)

                @block.gpsimd
                def _(pool):
                    pool.wait_ge(wmax_part, 1)
                    pool.partition_all_reduce(wmx[:, 1:2], wmx[:, 0:1], P, bass.bass_isa.ReduceOp.max).then_inc(wmax_all, 1)
                    pool.wait_ge(mhalf_set, 1)
                    pool.wait_ge(var_ready, 1)
                    pool.tensor_tensor(root[:, :], gvar[:, :], mhalf[:, :], ALU.pow).then_inc(root_ready, 1)

        weff = [sb(top, f"weff{k}", [P, 2, TAPS, C], F16) for k in range(2)]
        bw = [sb(top, f"bw{k}", [P, C], F16) for k in range(2)]
        e_max = sb(top, "e_max", [P, 1])
        with ExitStack() as pre:
            fh = sb(pre, "fh", [HALF, 2, NS1])
            u_sum = sb(pre, "u_sum", [HALF, 2, C, NG])
            norm_row = sb(pre, "norm_row", [P, 3, C])

            with ExitStack() as s2:
                xg = [sb(s2, f"xg{i}", [HALF, 2, CG, HALF]) for i in range(2)]
                rows = sb(s2, "rows", [HALF, H, 2, 2, C], F16)
                tmp = sb(s2, "tmp", [HALF, 4, 2 * H])
                ones = sb(s2, "ones", [C, P])
                ident = sb(s2, "ident", [C, C])
                diag = sb(s2, "diag", [C, 2, C])
                zrow = sb(s2, "zrow", [HALF, 2 * P * (SROWS - H - 1)], F16)
                fh_in = sem(s2, "fh_in")
                diag_ready = sem(s2, "diag_ready")
                spread_done = sem(s2, "spread_done")
                row_ready = sem(s2, "row_ready")
                zrow_ready = sem(s2, "zrow_ready")
                group_in = [sem(s2, f"group_in{i}") for i in range(2)]
                product = sem(s2, "product")
                scaled = sem(s2, "scaled")
                hi_made = sem(s2, "hi_made")
                split = sem(s2, "split")
                rows_out = sem(s2, "rows_out")
                zeros_out = sem(s2, "zeros_out")
                NGR = C // CG

                with nc.Block() as block:
                    @block.sync
                    def _(sp):
                        sp.dma_start(fh[:, :, :], t["fh"]).then_inc(fh_in, 16)
                        sp.dma_start(ident[:, :], t["ident"]).then_inc(fh_in, 16)
                        sp.wait_ge(zrow_ready, 1)
                        for wc in range(2):
                            sp.dma_start(scratch[wc, :, 0, :], zrow[:, 0:2 * P]).then_inc(zeros_out, 16)
                            sp.dma_start(scratch[wc, :, H + 1:SROWS, :].rearrange("w r e -> w (r e)"),
                                         zrow[:, :]).then_inc(zeros_out, 16)
                        for k in range(2 * NGR):
                            wc, g = k // NGR, k % NGR
                            if k >= 2:
                                sp.wait_ge(product, CG * (k - 1))
                            for hc in range(2):
                                src = x[0, g * CG:g * CG + CG, hc * HALF:hc * HALF + HALF, wc * HALF:wc * HALF + HALF]
                                sp.dma_start(xg[k % 2][:, hc, :, :], src.rearrange("c h w -> h c w"))\
                                  .then_inc(group_in[k % 2], 16)
                        sp.wait_ge(zeros_out, 64)

                    @block.tensor
                    def _(pe):
                        pe.wait_ge(diag_ready, 3)
                        pe.matmul(psum[7][:, 0:2 * C], ones[:, :], diag[:, :, :].rearrange("p a b -> p (a b)"),
                                  start=True, stop=True).then_inc(spread_done, 1)
                        pe.wait_ge(fh_in, 32)
                        pe.wait_ge(row_ready, 3)
                        for wc in range(2):
                            with pe.Fori(0, NGR // 2) as i:
                                for n in range(2):
                                    g = wc * NGR + 2 * i + n
                                    pe.wait_ge(group_in[n], 32 * (wc * (NGR // 2) + i) + 32)
                                    for c in range(CG):
                                        pe.wait_ge(scaled, CG * g + c + 1)
                                        for hc in range(2):
                                            mm = pe.matmul(psum[c][0:HALF, 0:NS1], xg[n][:, hc, c, :], fh[:, hc, :],
                                                           start=(hc == 0), stop=(hc == 1))
                                        mm.then_inc(product, 1)

                    @block.scalar
                    def _(act):
                        act.wait_ge(row_ready, 3)
                        for wc in range(2):
                            with act.Fori(0, NGR // 2) as i:
                                for n in range(2):
                                    g = wc * NGR + 2 * i + n
                                    for c in range(CG):
                                        act.wait_ge(product, CG * g + c + 1)
                                        act.wait_ge(split, CG * g + c + 1)
                                        ch = bass.ds((2 * i + n) * CG + c, 1)
                                        for p in range(2):
                                            act.activation(tmp[:, c % 4, p * H:p * H + H], psum[c][0:HALF, p * H:p * H + H],
                                                           ACT.Identity, scale=norm_row[0:HALF, 0, ch],
                                                           bias=norm_row[0:HALF, 1 + p, ch])
                                        act.activation(
                                            u_sum[:, wc, ch, :].rearrange("p a b -> p (a b)"), psum[c][0:HALF, 2 * H:NS1],
                                            ACT.Identity).then_inc(scaled, 1)

                    @block.vector
                    def _(dve):
                        dve.memset(zrow[:, :], 0.0).then_inc(zrow_ready, 1)
                        dve.memset(diag[:, 0, 0:1], 0.0).then_inc(scaled, CG)
                        dve.memset(diag[:, 1, 0:1], 0.0).then_inc(split, 4)
                        dve.wait_ge(scaled, CG)
                        dve.wait_ge(split, 4)
                        dve.memset(ones[:, :], 1.0).then_inc(diag_ready, 1)
                        dve.wait_ge(fh_in, 32)
                        for k in range(2):
                            dve.tensor_scalar(diag[:, k, :], ident[:, :], norm[0:C, k:k + 1], None, ALU.mult)\
                               .then_inc(diag_ready, 1)
                        dve.wait_ge(spread_done, 1)
                        dve.tensor_copy(norm_row[:, 0, :], psum[7][:, 0:C]).then_inc(row_ready, 1)
                        dve.tensor_scalar(norm_row[:, 1, :], psum[7][:, C:2 * C], SUM_L, None, ALU.mult).then_inc(row_ready, 1)
                        dve.tensor_scalar(norm_row[:, 2, :], psum[7][:, C:2 * C], SUM_H, None, ALU.mult).then_inc(row_ready, 1)
                        for wc in range(2):
                            if wc:
                                dve.wait_ge(rows_out, 16)
                            with dve.Fori(0, NGR // 2) as i:
                                for n in range(2):
                                    g = wc * NGR + 2 * i + n
                                    for c in range(CG):
                                        dve.wait_ge(scaled, CG * g + c + 1 + CG)
                                        ch = bass.ds((2 * i + n) * CG + c, 1)
                                        v = tmp[:, c % 4, :].rearrange("w (p r) -> w r p", p=2)
                                        hi = rows[:, :, 0, :, ch].rearrange("w r p a -> w r (p a)")
                                        lo = rows[:, :, 1, :, ch].rearrange("w r p a -> w r (p a)")
                                        dve.tensor_copy(hi, v).then_inc(hi_made, 1)
                                        dve.wait_ge(hi_made, CG * g + c + 1)
                                        dve.tensor_tensor(lo, v, hi, ALU.subtract).then_inc(split, 1)

                    @block.gpsimd
                    def _(pool):
                        for wc in range(2):
                            pool.wait_ge(split, C * (wc + 1) + 4)
                            pool.dma_start(scratch[wc, :, 1:H + 1, :].rearrange("w r e -> w (r e)"),
                                           rows[:, :, :, :, :].rearrange("w r k p c -> w (r k p c)")).then_inc(rows_out, 16)
                        pool.wait_ge(rows_out, 32)

            with ExitStack() as s3:
                names = ["gw", "of_mean", "pick", "dsum", "wd_low", "wd_high", "bd", "w1_low", "w1_high",
                         "w2_low", "w2_high", "wa_low", "wa_high", "ba", "enc_low", "enc_high", "b_enc"]
                c3 = {n: sb(s3, n, list(t[n].shape)) for n in names}
                tn = sb(s3, "tn", [C, NG * NG])
                tc = sb(s3, "tc", [C, NG * NG])
                sk = sb(s3, "sk", [C, 4, NK])
                neg_m = sb(s3, "neg_m", [P, 1])
                junk = sb(s3, "junk", [96, 3, NK])
                yd = sb(s3, "yd", [96, 3])
                yb = sb(s3, "yb", [96, 3])
                y = sb(s3, "y", [96, 3])
                z = sb(s3, "z", [12, 2])
                sg = sb(s3, "sg", [96, 3])
                bs = sb(s3, "bs", [96, 3])
                was_low = sb(s3, "was_low", [C, C])
                was_high = sb(s3, "was_high", [96, 2, 3 * C])
                e32 = sb(s3, "e32", [P, 2, TAPS * C])
                en = sb(s3, "en", [P, 2, TAPS * C])
                brow = sb(s3, "brow", [1, TAPS * C])
                b32 = sb(s3, "b32", [P, C])
                bn = sb(s3, "bn", [P, C])
                emx = sb(s3, "emx", [P, 4])
                einv = sb(s3, "einv", [P, 1])
                in3 = sem(s3, "in3")
                dch = sem(s3, "dch")
                t_done = sem(s3, "t_done")
                s_ready = sem(s3, "s_ready")
                y_done = sem(s3, "y_done")
                y_ready = sem(s3, "y_ready")
                z_done = sem(s3, "z_done")
                z_ready = sem(s3, "z_ready")
                sc_done = sem(s3, "sc_done")
                sig_done = sem(s3, "sig_done")
                was_ready = sem(s3, "was_ready")
                e_done = sem(s3, "e_done")
                brow_ready = sem(s3, "brow_ready")
                b32_in = sem(s3, "b32_in")
                emax_part = sem(s3, "emax_part")
                emax_all = sem(s3, "emax_all")
                HN = TAPS * C // 2

                with nc.Block() as block:
                    @block.sync
                    def _(sp):
                        for n in names:
                            sp.dma_start(c3[n][(slice(None),) * len(t[n].shape)], t[n]).then_inc(in3, 16)
                        sp.wait_ge(brow_ready, 2)
                        sp.dma_start(b32[0:TAPS, :], brow[0:1, :].rearrange("a (t e) -> a t e", t=TAPS)).then_inc(b32_in, 16)

                    @block.tensor
                    def _(pe):
                        pe.wait_ge(in3, 16 * len(names))
                        for u in range(NG):
                            for wc in range(2):
                                mm = pe.matmul(psum[0][0:C, u * NG:u * NG + NG], u_sum[:, wc, :, u], c3["gw"][:, wc, :],
                                               start=(wc == 0), stop=(wc == 1))
                        mm.then_inc(t_done, 1)
                        pe.wait_ge(s_ready, 1)
                        pe.matmul(psum[1][0:C, 0:NK], c3["wd_low"][:, :], sk[:, 0, :], start=True, stop=True)
                        for g in range(2):
                            for j in range(3):
                                mm = pe.matmul(psum[1][0:96, NK * (1 + g):NK * (2 + g)],
                                               c3["wd_high"][:, j, 96 * g:96 * g + 96], sk[:, SUBBAND[j], :],
                                               start=(j == 0), stop=(j == 2))
                        mm.then_inc(y_done, 1)
                        pe.wait_ge(y_ready, 1)
                        pe.matmul(psum[2][0:4, 0:1], c3["w1_low"][:, :], y[0:C, 0:1], start=True, stop=True)
                        for g in range(2):
                            mm = pe.matmul(psum[2][0:12, 1:2], c3["w1_high"][:, g, :], y[:, 1 + g:2 + g],
                                           start=(g == 0), stop=(g == 1))
                        mm.then_inc(z_done, 1)
                        pe.wait_ge(z_ready, 2)
                        pe.matmul(psum[3][0:C, 0:1], c3["w2_low"][:, :], z[0:4, 0:1], start=True, stop=True)
                        for g in range(2):
                            mm = pe.matmul(psum[3][0:96, 1 + g:2 + g], c3["w2_high"][:, 96 * g:96 * g + 96], z[0:12, 1:2],
                                           start=True, stop=True)
                        mm.then_inc(sc_done, 1)
                        pe.wait_ge(was_ready, 6)
                        for sw in range(2):
                            for n in range(2):
                                ps = psum[4 + 2 * sw + n]
                                cols = slice(n * HN, n * HN + HN)
                                for sh in range(2):
                                    o = ps[C * sh:C * sh + C, 0:HN]
                                    sub = 2 * sh + sw
                                    if sub == 0:
                                        pe.matmul(o, was_low[:, :], c3["enc_low"][:, cols], start=True, stop=True)
                                        continue
                                    for g in range(2):
                                        pe.matmul(o, was_high[:, g, C * (sub - 1):C * sub], c3["enc_high"][:, g, cols],
                                                  start=(g == 0), stop=(g == 1))
                        for n in range(2):
                            cols = slice(n * HN, n * HN + HN)
                            o = psum[n][0:1, 0:HN]
                            pe.matmul(o, bs[0:C, 0:1], c3["enc_low"][:, cols], start=True, stop=False)
                            for g in range(2):
                                mm = pe.matmul(o, bs[:, 1 + g:2 + g], c3["enc_high"][:, g, cols], start=False, stop=(g == 1))
                        mm.then_inc(e_done, 1)

                    @block.scalar
                    def _(act):
                        act.wait_ge(sc_done, 1)
                        act.activation(sg[0:C, 0:1], psum[3][0:C, 0:1], ACT.Sigmoid).then_inc(sig_done, 1)
                        act.activation(sg[:, 1:3], psum[3][0:96, 1:3], ACT.Sigmoid).then_inc(sig_done, 1)

                    @block.vector
                    def _(dve):
                        count = [0]

                        def step(ins):
                            count[0] += 1
                            ins.then_inc(dch, 1)
                            dve.wait_ge(dch, count[0])
                        step(dve.memset(yd[:, :], 0.0))
                        step(dve.memset(b32[:, :], 0.0))
                        dve.wait_ge(in3, 16 * len(names))
                        step(dve.tensor_scalar(neg_m[:, :], gmean[:, :], -1.0, None, ALU.mult))
                        dve.wait_ge(t_done, 1)
                        step(dve.scalar_tensor_tensor(tc[:, :], c3["of_mean"][:, :], neg_m[0:C, 0:1], psum[0][0:C, 0:NG * NG],
                                                      ALU.mult, ALU.add))
                        step(dve.tensor_scalar(tn[:, :], tc[:, :], norm[0:C, 0:1], None, ALU.mult))
                        tv = tn[:, :].rearrange("c (a u b v) -> c a u b v", a=2, u=NF, b=2)
                        so = sk[:, :, :].rearrange("c (a b) k -> c a b k", a=2)
                        for k in range(NK):
                            ins = dve.tensor_copy(so[:, :, :, k], tv[:, :, MX[k], :, MY[k]])
                        count[0] += 1
                        ins.then_inc(dch, 1)
                        dve.wait_ge(dch, count[0])
                        dve.tensor_tensor(yb[:, :], c3["bd"][:, :], c3["dsum"][:, :], ALU.mult).then_inc(s_ready, 1)
                        dve.wait_ge(s_ready, 1)
                        dve.wait_ge(y_done, 1)
                        for g in range(3):
                            m = C if g == 0 else 96
                            step(dve.tensor_tensor_reduce(junk[0:m, g, :], psum[1][0:m, NK * g:NK * g + NK],
                                                          c3["pick"][0:m, g, :], 1.0, 0.0, ALU.mult, ALU.add,
                                                          yd[0:m, g:g + 1]))
                        dve.tensor_tensor(y[:, :], yd[:, :], yb[:, :], ALU.add).then_inc(y_ready, 1)
                        dve.wait_ge(z_done, 1)
                        dve.tensor_scalar(z[0:4, 0:1], psum[2][0:4, 0:1], 0.0, None, ALU.max).then_inc(z_ready, 1)
                        dve.tensor_scalar(z[0:12, 1:2], psum[2][0:12, 1:2], 0.0, None, ALU.max).then_inc(z_ready, 1)
                        dve.wait_ge(sig_done, 2)
                        dve.tensor_scalar(was_low[:, :], c3["wa_low"][:, :], sg[0:C, 0:1], None, ALU.mult).then_inc(was_ready, 1)
                        for g in range(2):
                            dve.tensor_scalar(was_high[:, g, :], c3["wa_high"][:, g, :], sg[:, 1 + g:2 + g], None, ALU.mult)\
                               .then_inc(was_ready, 1)
                        dve.tensor_tensor(bs[0:C, 0:1], c3["ba"][0:C, 0:1], sg[0:C, 0:1], ALU.mult).then_inc(was_ready, 1)
                        dve.tensor_tensor(bs[:, 1:3], c3["ba"][:, 1:3], sg[:, 1:3], ALU.mult).then_inc(was_ready, 1)
                        dve.memset(emx[:, :], 0.0).then_inc(was_ready, 1)
                        dve.wait_ge(e_done, 1)
                        for sw in range(2):
                            for n in range(2):
                                ins = dve.tensor_copy(e32[:, sw, n * HN:n * HN + HN], psum[4 + 2 * sw + n][:, 0:HN])
                        step(ins)
                        dve.tensor_copy(brow[0:1, 0:HN], psum[0][0:1, 0:HN]).then_inc(brow_ready, 1)
                        step(dve.tensor_copy(brow[0:1, HN:2 * HN], psum[1][0:1, 0:HN]))
                        mid = slice(4 * C, 5 * C)
                        dve.wait_ge(brow_ready, 1)
                        dve.tensor_tensor(brow[0:1, mid], brow[0:1, mid], c3["b_enc"][0:1, :], ALU.add).then_inc(brow_ready, 1)
                        dve.wait_ge(b32_in, 16)
                        dve.wait_ge(was_ready, 6)
                        step(dve.tensor_reduce(emx[:, 0:1], e32[:, :, :].rearrange("p a b -> p (a b)"), AX.X, ALU.max,
                                               apply_absolute_value=True))
                        step(dve.tensor_reduce(emx[:, 1:2], b32[:, :], AX.X, ALU.max, apply_absolute_value=True))
                        dve.tensor_reduce(emx[:, 2:3], emx[:, 0:2], AX.X, ALU.max).then_inc(emax_part, 1)
                        dve.wait_ge(emax_all, 1)
                        step(dve.tensor_scalar(e_max[:, :], emx[:, 3:4], 1e-30, None, ALU.max))
                        step(dve.reciprocal(einv[:, :], e_max[:, :]))
                        step(dve.tensor_scalar(en[:, :, :], e32[:, :, :], einv[:, 0:1], None, ALU.mult))
                        step(dve.tensor_scalar(bn[:, :], b32[:, :], einv[:, 0:1], None, ALU.mult))
                        ev = en[:, :, :].rearrange("p s (t e) -> p (s t) e", t=TAPS)
                        wv = [w[:, :, :, :].rearrange("p s t e -> p (s t) e") for w in weff]
                        step(dve.tensor_copy(wv[0], ev))
                        step(dve.tensor_copy(bw[0][:, :], bn[:, :]))
                        step(dve.tensor_tensor(wv[1], ev, wv[0], ALU.subtract))
                        step(dve.tensor_tensor(bw[1][:, :], bn[:, :], bw[0][:, :], ALU.subtract))

                    @block.gpsimd
                    def _(pool):
                        pool.wait_ge(emax_part, 1)
                        pool.partition_all_reduce(emx[:, 3:4], emx[:, 2:3], P, bass.bass_isa.ReduceOp.max)\
                            .then_inc(emax_all, 1)

        e_map = sb(top, "e_map", [P, HALF * W])
        encoder(nc, t, scratch, psum, sb, sem, weff, bw, e_max, b_id, e_map)
        main(nc, x, out, psum, sb, sem, e_map, partner, records, mv, quad, gsum, gvar, mhalf, root, norm, newt, w_hi, w_lo,
             w_max, combine, commit)


def encoder(nc, t, scratch, psum, sb, sem, weff, bw, e_max, b_id, e_map):
    with ExitStack() as s4:
        fw = sb(s4, "fw", [HALF, 2, 2, 2 * W], F16)
        s_in = [sb(s4, f"s_in{i}", [HALF, 2, 2, ER, 2 * P], F16) for i in range(2)]
        s_halo = sb(s4, "s_halo", [HALF, 2, 2, 2, 2 * P], F16)
        d = [sb(s4, f"d{i}", [P, 4, EH, 2, WP], F16) for i in range(2)]
        inside = [sb(s4, f"inside{i}", [P, 2, ER * W], F16) for i in range(2)]
        lin = sb(s4, "lin", [P, 2, NT])
        leak = sb(s4, "leak", [P, 2, NT])
        fw_in = sem(s4, "fw_in")
        halo_in = sem(s4, "halo_in")
        step_in = [sem(s4, f"step_in{i}") for i in range(2)]
        inside_in = [sem(s4, f"inside_in{i}") for i in range(2)]
        pads_set = sem(s4, "pads_set")
        gen_done = sem(s4, "gen_done")
        hi_done = sem(s4, "hi_done")
        lo_done = sem(s4, "lo_done")
        carried = sem(s4, "carried")
        conv_done = sem(s4, "conv_done")
        lin_done = sem(s4, "lin_done")
        leak_done = sem(s4, "leak_done")
        map_done = sem(s4, "map_done")
        FIRST = 2 * EH

        with nc.Block() as block:
            @block.sync
            def _(sp):
                def load(buf, row0, n, signal):
                    for wc in range(2):
                        for s in range(2):
                            sp.dma_start(buf[:, wc, s, :, :].rearrange("w r e -> w (r e)"),
                                         scratch[wc, :, bass.ds(row0 + HALF * s, n), :].rearrange("w r e -> w (r e)"))\
                              .then_inc(signal, 16)
                sp.dma_start(fw[:, :, :, :], t["fw"]).then_inc(fw_in, 16)
                load(s_halo, 0, 2, halo_in)
                load(s_in[0], 2, ER, step_in[0])
                def load_inside(n, step):
                    for s in range(2):
                        sp.dma_start(inside[n][0:TAPS, s, :], t["inside"][:, bass.ds((ER * step + HALF * s) * W, ER * W)])\
                          .then_inc(inside_in[n], 16)
                sp.wait_ge(pads_set, 6)
                load_inside(0, 0)
                with sp.Fori(0, NE // 2) as i:
                    for n in range(2):
                        step = 2 * i + n
                        m = (n + 1) % 2
                        sp.wait_ge(gen_done, FIRST + 8 * step)
                        load(s_in[m], ER * (step + 1) + 2, ER, step_in[m])
                        sp.wait_ge(conv_done, 2 * step + 1)
                        load_inside(m, step + 1)
                sp.wait_ge(inside_in[0], 32 * (NE // 2 + 1))

            @block.tensor
            def _(pe):
                def gen(tile, lhs):
                    k = 0
                    for wc in range(2):
                        for a, b in ((0, 0), (0, 1), (1, 0)):
                            mm = pe.matmul(psum[tile % 4][:, 0:NT], lhs[:, wc, P * a:P * a + P], fw[:, wc, b, :],
                                           start=(k == 0), stop=(k == 5))
                            k += 1
                    mm.then_inc(gen_done, 1)

                def conv(step, n, q):
                    o = psum[4 + 2 * n + q]
                    pieces = [(weff[a][:, sw, 3 * ky + kx, :], b, ky, kx, sw)
                              for a, b in ((0, 0), (0, 1), (1, 0)) for sw in range(2) for ky in range(3) for kx in range(3)]
                    for k, (w, b, ky, kx, sw) in enumerate(pieces):
                        for s in range(2):
                            pe.matmul(o[C * s:C * s + C, 0:NT], w,
                                      d[n][:, 2 * s + b, 2 * q + ky:2 * q + ky + 2, sw, kx:kx + W], start=(k == 0), stop=False)
                    for a in range(2):
                        for s in range(2):
                            mm = pe.matmul(o[C * s:C * s + C, 0:NT], bw[a][:, :],
                                           inside[n][:, s, 2 * q * W:2 * q * W + NT], start=False, stop=(a == 1))
                    mm.then_inc(conv_done, 1)

                pe.wait_ge(fw_in, 16)
                pe.wait_ge(halo_in, 64)
                pe.wait_ge(step_in[0], 64)
                pe.wait_ge(pads_set, 6)
                for k in range(FIRST):
                    if k >= 4:
                        pe.wait_ge(lo_done, k - 3)
                    s, r = k % 2, k // 2
                    gen(k, s_halo[:, :, s, r, :] if r < 2 else s_in[0][:, :, s, r - 2, :])
                with pe.Fori(0, NE // 2) as i:
                    for n in range(2):
                        step = 2 * i + n
                        m = (n + 1) % 2
                        pe.wait_ge(step_in[m], 64 * (i + 1) + (0 if n == 0 else 64))
                        for k in range(8):
                            pe.wait_ge(lo_done, FIRST + 8 * step + k - 3)
                            gen(k, s_in[m][:, :, k % 2, k // 2, :])
                        pe.wait_ge(lo_done, FIRST + 8 * step)
                        pe.wait_ge(carried, step + 1)
                        pe.wait_ge(inside_in[n], 32 * i + 32)
                        pe.wait_ge(leak_done, 2 * step + 1)
                        for q in range(2):
                            conv(step, n, q)

            @block.scalar
            def _(act):
                def hi(tile, k, slot, s, r):
                    act.wait_ge(gen_done, tile + 1)
                    act.copy(d[slot][:, 2 * s, r, :, 1:1 + W], psum[k % 4][:, 0:NT].rearrange("p (a w) -> p a w", a=2))\
                       .then_inc(hi_done, 1)

                act.wait_ge(pads_set, 6)
                for k in range(FIRST):
                    hi(k, k, 0, k % 2, k // 2)
                with act.Fori(0, NE // 2) as i:
                    for n in range(2):
                        step = 2 * i + n
                        m = (n + 1) % 2
                        act.wait_ge(conv_done, 2 * step + 1)
                        for k in range(8):
                            hi(FIRST + 8 * step + k, k, m, k % 2, 2 + k // 2)
                        for q in range(2):
                            act.wait_ge(conv_done, 2 * step + q + 2)
                            act.wait_ge(leak_done, 2 * step + q + 1)
                            act.activation(lin[:, q, :], psum[4 + 2 * n + q][:, 0:NT], ACT.Identity, scale=e_max[:, 0:1])\
                               .then_inc(lin_done, 1)

            @block.vector
            def _(dve):
                def lo(tile, k, slot, s, r):
                    dve.wait_ge(hi_done, tile + 1)
                    dve.tensor_tensor(d[slot][:, 2 * s + 1, r, :, 1:1 + W], psum[k % 4][:, 0:NT].rearrange("p (a w) -> p a w", a=2),
                                      d[slot][:, 2 * s, r, :, 1:1 + W], ALU.subtract).then_inc(lo_done, 1)

                for n in range(2):
                    dv = d[n][:, :, :, :, :].rearrange("p a r s w -> p (a r s) w")
                    dve.memset(dv[:, :, 0:1], 0.0).then_inc(pads_set, 1)
                    dve.memset(dv[:, :, WP - 1:WP], 0.0).then_inc(pads_set, 1)
                    dve.memset(inside[n][:, :, :], 0.0).then_inc(pads_set, 1)
                for k, counter in enumerate((conv_done, carried, leak_done, map_done)):
                    dve.memset(leak[:, 0, k:k + 1], 0.0).then_inc(counter, 1)
                dve.wait_ge(pads_set, 6)
                dve.wait_ge(leak_done, 1)
                dve.wait_ge(map_done, 1)
                dve.wait_ge(fw_in, 16)
                for k in range(FIRST):
                    lo(k, k, 0, k % 2, k // 2)
                with dve.Fori(0, NE // 2) as i:
                    for n in range(2):
                        step = 2 * i + n
                        m = (n + 1) % 2
                        dve.wait_ge(conv_done, 2 * step + 1)
                        dve.wait_ge(lo_done, FIRST + 8 * step)
                        dve.tensor_copy(d[m][:, :, 0:2, :, :].rearrange("p a r s w -> p a (r s w)"),
                                        d[n][:, :, ER:EH, :, :].rearrange("p a r s w -> p a (r s w)")).then_inc(carried, 1)
                        for k in range(8):
                            lo(FIRST + 8 * step + k, k, m, k % 2, 2 + k // 2)
                        for q in range(2):
                            dve.wait_ge(lin_done, 2 * step + q + 1)
                            dve.wait_ge(map_done, 2 * step + q + 1)
                            dve.scalar_tensor_tensor(leak[:, q, :], lin[:, q, :], 0.01, lin[:, q, :], ALU.mult, ALU.max)\
                               .then_inc(leak_done, 1)
                            dve.wait_ge(leak_done, 2 * step + q + 2)
                            dve.tensor_scalar(e_map[:, bass.ds((ER * step + 2 * q) * W, NT)], leak[:, q, :], b_id[:, 0:1], None,
                                              ALU.add).then_inc(map_done, 1)


def main(nc, x, out, psum, sb, sem, e_map, partner, records, mv, quad, gsum, gvar, mhalf, root, norm, newt, w_hi, w_lo,
         w_max, combine, commit):
    with ExitStack() as s5:
        xs = [sb(s5, f"xs{i}", [P, RH * W]) for i in range(XS)]
        xn = sb(s5, "xn", [P, RH * W])
        same = [[sb(s5, f"same{i}{s}", [P, RH, WP], F16) for s in range(2)] for i in range(2)]
        next_ = [[sb(s5, f"next{i}{s}", [P, RH, WP], F16) for s in range(2)] for i in range(2)]
        stage = sb(s5, "stage", [P, PAIRS, NT])
        sx = [sb(s5, f"sx{i}", [P, SC]) for i in range(2)]

        x_in = [sem(s5, f"x_in{i}") for i in range(XS)]
        x_free = [sem(s5, f"x_free{i}") for i in range(XS)]
        stat_in = [sem(s5, f"stat_in{i}") for i in range(2)]
        stat_used = sem(s5, "stat_used")
        tiles = sem(s5, "tiles")
        act_prep = sem(s5, "act_prep")
        dve_prep = sem(s5, "dve_prep")
        split_edge = sem(s5, "split_edge")
        evac = sem(s5, "evac")
        added = sem(s5, "added")
        normed = sem(s5, "normed")
        chain = sem(s5, "chain")
        commits = sem(s5, "commits")
        aggregated = sem(s5, "aggregated5")
        partners_done = sem(s5, "partners_done5")
        var_ready = sem(s5, "var_ready5")
        root_ready = sem(s5, "root_ready5")
        TOP, BOTTOM, IN = range(3)

        def edge(i):
            return [(NB * i, 2, BOTTOM, NB - 1), (NB * i + 1, 3, TOP, 0)]

        def inner(i, it, j):
            return NB * i + 2 + 4 * it + j, j, IN, 1 + 4 * it + j

        def uses(i, it, slot, kind):
            return (INNER + 1) * i + (0 if kind != IN else 1 + it) if slot >= 2 else INNER * i + it

        with nc.Block() as block:
            @block.sync
            def _(sp):
                def load(i, it, n, slot, kind, band):
                    u = uses(i, it, slot, kind)
                    top_row = band * R if isinstance(band, int) else sp.snap(band * R)
                    sp.wait_ge(x_free[slot], 32 * u + 32)
                    for s in (1, 0):
                        lo_row, hi_row = 0, RH
                        if kind == TOP and s == 0:
                            lo_row = 1
                        if kind == BOTTOM and s == 1:
                            hi_row = RH - 1
                        rows = hi_row - lo_row
                        src = x[bass.ds(i, 1), :, bass.ds(HALF * s + top_row - 1 + lo_row, rows), :]
                        sp.dma_start(xs[slot][C * s:C * s + C, lo_row * W:hi_row * W],
                                     src.rearrange("a c h w -> (a c) (h w)")).then_inc(x_in[slot], 16)

                def load_stats(nxt, k, row0, rows):
                    sp.wait_ge(stat_used, k + 1)
                    for s in range(2):
                        src = x[bass.ds(nxt, 1), :, bass.ds(HALF * s + row0, rows), :]
                        sp.dma_start(sx[row0_slot[0]][C * s:C * s + C, 0:rows * W],
                                     src.rearrange("a c h w -> (a c) (h w)")).then_inc(stat_in[row0_slot[0]], 16)
                    row0_slot[0] ^= 1

                row0_slot = [0]
                with sp.Fori(0, B) as i:
                    nxt = sp.snap((i + 1) % B)
                    for k, (n, slot, kind, band) in enumerate(edge(i)):
                        load(i, 0, n, slot, kind, band)
                        load_stats(nxt, 20 * i + k, SR_EDGE * k, SR_EDGE)
                    with sp.Fori(0, INNER) as it:
                        for j in range(4):
                            load(i, it, *inner(i, it, j))
                            for c in range(2 * j, 2 * j + 2) if j < 3 else ():
                                load_stats(nxt, 20 * i + 2 + 6 * it + c, 2 * SR_EDGE + SR_IN * (6 * it + c), SR_IN)

            @block.scalar
            def _(act):
                def prep(n, slot, kind, band, i, it):
                    p = 0 if slot % 2 == 0 else 1
                    u = uses(i, it, slot, kind)
                    act.wait_ge(x_in[slot], 32 * u + 32)
                    act.wait_ge(tiles, PAIRS * n + PAIRS)
                    v = xs[slot][:, :].rearrange("p (r w) -> p r w", w=W)

                    def part(dst, lanes, r0, r1):
                        return act.activation(dst, v[lanes, r0:r1, :], ACT.Identity, scale=norm[lanes, 0:1], bias=norm[lanes, 1:2])
                    up, dn = slice(0, C), slice(C, P)
                    part(same[p][0][up, :, 1:1 + W], up, 0, RH).then_inc(act_prep, 1)
                    part(same[p][1][dn, :, 1:1 + W], dn, 0, RH).then_inc(act_prep, 1)
                    act.wait_ge(dve_prep, n + 1)
                    act.activation(xn[:, :], xs[slot][:, :], ACT.Identity, scale=norm[:, 0:1], bias=norm[:, 1:2]).then_inc(act_prep, 1)
                    part(next_[p][0][dn, 0:RH - 1, 1:1 + W], up, 1, RH).then_inc(act_prep, 1)
                    part(next_[p][1][up, 0:RH - 1, 1:1 + W], dn, 1, RH).then_inc(act_prep, 1)

                with act.Fori(0, B) as i:
                    act.wait_ge(normed, i + 1)
                    for e in edge(i):
                        prep(*e, i, 0)
                    with act.Fori(0, INNER) as it:
                        for j in range(4):
                            prep(*inner(i, it, j), i, it)

            @block.vector
            def _(dve):
                up, dn = slice(0, C), slice(C, P)

                def prep(n, slot, kind, i):
                    p = slot % 2
                    dve.wait_ge(tiles, PAIRS * n + PAIRS)
                    dve.wait_ge(act_prep, 5 * n + 3)
                    dve.tensor_copy(next_[p][0][up, 0:RH - 1, :], same[p][0][up, 0:RH - 1, :])
                    dve.tensor_copy(next_[p][1][dn, 0:RH - 1, :], same[p][1][dn, 0:RH - 1, :])
                    dve.wait_ge(act_prep, 5 * n + 4)
                    nv = xn[:, :].rearrange("p (r w) -> p r w", w=W)
                    dve.tensor_tensor(same[p][0][dn, :, 1:1 + W], nv[up, :, :], same[p][0][up, :, 1:1 + W], ALU.subtract)
                    last = dve.tensor_tensor(same[p][1][up, :, 1:1 + W], nv[dn, :, :], same[p][1][dn, :, 1:1 + W], ALU.subtract)
                    if kind != IN:
                        last.then_inc(split_edge, 1)
                        dve.wait_ge(act_prep, 5 * n + 6)
                        dve.wait_ge(split_edge, 2 * i + (1 if kind == BOTTOM else 2))
                        if kind == TOP:
                            dve.memset(same[p][0][:, 0, :], 0.0)
                            last = dve.memset(next_[p][0][up, 0, :], 0.0)
                        else:
                            dve.memset(same[p][1][:, RH - 1, :], 0.0)
                            last = dve.memset(next_[p][1][up, RH - 2, :], 0.0)
                    last.then_inc(dve_prep, 1)

                def read_out(n, slot, band, parity):
                    for q in range(PAIRS):
                        dve.wait_ge(tiles, PAIRS * n + PAIRS + q + 1)
                        dve.wait_ge(added, PAIRS * n + q + 1)
                        dve.scalar_tensor_tensor(stage[:, q, :], psum[PAIRS * parity + q][:, 0:NT], w_max[:, 0:1],
                                                 e_map[:, bass.ds((band * R + 2 * q) * W, NT)], ALU.mult, ALU.add)\
                           .then_inc(evac, 1)

                def take_stats(turn, rec0, rows):
                    m = slot_s[0]
                    dve.wait_ge(stat_in[m], 32 * turn + 32)
                    for r in range(rows // 2):
                        ins = dve.bn_stats(records[:, bass.ds(rec0 + r, 1), :].rearrange("p a b -> p (a b)"),
                                           sx[m][:, r * NT:r * NT + NT])
                    ins.then_inc(stat_used, 1)
                    slot_s[0] ^= 1

                slot_s = [0]
                for p in range(2):
                    for s in range(2):
                        for buf in (same[p][s], next_[p][s]):
                            last = dve.memset(buf[:, :, :], 0.0)
                    last.then_inc(tiles, PAIRS)
                dve.wait_ge(tiles, 2 * PAIRS)
                dve.memset(newt[:, 0:1], 0.0).then_inc(stat_used, 2)
                for k, counter in enumerate((dve_prep, act_prep, root_ready, evac)):
                    dve.memset(quad[:, k, :], 0.0).then_inc(counter, 1)
                dve.wait_ge(stat_used, 2)
                dve.wait_ge(evac, 1)
                with dve.Fori(0, B) as i:
                    dve.wait_ge(act_prep, 5 * NB * i + 1)
                    dve.wait_ge(root_ready, INNER * i + 1)
                    commit(dve, commits, 5 * i)
                    dve.tensor_copy(gsum[:, 0:1], norm[:, 0:1]).then_inc(normed, 1)
                    for k, (n, slot, kind, band) in enumerate(edge(i)):
                        prep(n, slot, kind, i)
                        take_stats(10 * i, k * SR_EDGE // 2, SR_EDGE)
                        read_out(n, slot - 1, NB - 2 if k == 0 else NB - 1, (slot - 1) % 2)
                    with dve.Fori(0, INNER) as it:
                        for j in range(4):
                            n, slot, kind, band = inner(i, it, j)
                            if j == 3:
                                dve.wait_ge(stat_used, 20 * i + 2 + 6 * it + 6 + 2)
                            prep(n, slot, kind, i)
                            if j == 3:
                                dve.bn_aggr(mv[:, :], records[:, :, :].rearrange("p a b -> p (a b)")).then_inc(aggregated, 1)
                            for c in range(2 * j, 2 * j + 2) if j < 3 else ():
                                take_stats(10 * i + 1 + 3 * it + c // 2, 2 + 3 * (6 * it + c), SR_IN)
                            read_out(n, slot - 1, band - 1, (slot - 1) % 2)
                            if j == 3:
                                dve.wait_ge(partners_done, INNER * i + it + 1)
                                dve.wait_ge(root_ready, INNER * i + it + 1)
                                combine(dve, chain, 8 * (INNER * i + it), psum[7][:, NT:NT + 6].rearrange("p (a b) -> p a b", a=3))
                                dve.tensor_scalar(gvar[:, :], gsum[:, 1:2], 0.25, EPS, ALU.mult, ALU.add).then_inc(var_ready, 1)
                read_out(NB * B, 3, NB - 2, 1)

            @block.tensor
            def _(pe):
                def conv(n, p, last_tile_waits=None):
                    pe.wait_ge(act_prep, 5 * n + 6)
                    pe.wait_ge(dve_prep, n + 2)
                    pe.wait_ge(evac, PAIRS * n + 1)
                    for q in range(PAIRS):
                        if q == PAIRS - 1 and last_tile_waits is not None:
                            pe.wait_ge(*last_tile_waits)
                        o = psum[PAIRS * p + q]
                        y = 2 * q
                        for k in range(15):
                            for s in range(2):
                                if k < 9:
                                    ky, kx = k // 3, k % 3
                                    w, v, r = w_hi[:, k, :], same[p][s], y + ky
                                else:
                                    kx = (k - 9) % 3
                                    w, v, r = w_lo[s][:, k - 9, :], next_[p][s], y + (k >= 12)
                                mm = pe.matmul(o[C * s:C * s + C, 0:NT], w, v[:, r:r + 2, kx:kx + W],
                                               start=(k == 0), stop=(k == 14))
                        mm.then_inc(tiles, 1)

                with pe.Fori(0, B) as i:
                    for n, slot, kind, band in edge(i):
                        conv(n, slot % 2)
                    with pe.Fori(0, INNER) as it:
                        for j in range(4):
                            n, slot, kind, band = inner(i, it, j)
                            if j == 3:
                                pe.wait_ge(evac, PAIRS * n + 1)
                                pe.wait_ge(aggregated, INNER * i + it + 1)
                                for k in range(3):
                                    mm = pe.matmul(psum[7][:, NT + 2 * k:NT + 2 * k + 2], partner[:, k, :], mv[:, :],
                                                   start=True, stop=True)
                                mm.then_inc(partners_done, 1)
                            conv(n, slot % 2, (var_ready, INNER * i + it + 1) if j == 3 else None)

            @block.gpsimd
            def _(pool):
                def finish(n, slot, band, i):
                    v = xs[slot][:, W:(R + 1) * W]
                    for q in range(PAIRS):
                        pool.wait_ge(evac, PAIRS * n + PAIRS + q + 2)
                        pool.tensor_tensor(v[:, q * NT:q * NT + NT], stage[:, q, :], v[:, q * NT:q * NT + NT], ALU.add)\
                            .then_inc(added, 1)
                    pool.wait_ge(added, 3 * PAIRS + PAIRS * n)
                    for s in range(2):
                        dst = out[bass.ds(i, 1), :, bass.ds(HALF * s + R * band, R), :]
                        pool.dma_start(dst.rearrange("a c h w -> (a c) (h w)"), v[C * s:C * s + C, :]).then_inc(x_free[slot], 16)

                for s in range(XS):
                    for h in range(2):
                        pool.dma_start(xs[s][C * h:C * h + C, :], x[0, :, 0:RH, :].rearrange("c h w -> c (h w)"))\
                            .then_inc(x_free[s], 16)
                pool.memset(stage[:, :, :], 0.0).then_inc(added, 2 * PAIRS)
                pool.wait_ge(added, 2 * PAIRS)
                with pool.Fori(0, B) as i:
                    for n, slot, kind, band in edge(i):
                        finish(n, slot, band, i)
                    with pool.Fori(0, INNER) as it:
                        for j in range(4):
                            n, slot, kind, band = inner(i, it, j)
                            finish(n, slot, band, i)
                            if j == 2:
                                pool.wait_ge(var_ready, INNER * i + it + 1)
                                pool.tensor_tensor(root[:, :], gvar[:, :], mhalf[:, :], ALU.pow).then_inc(root_ready, 1)
                for s in range(XS):
                    pool.wait_ge(x_free[s], 32 * (B * (INNER + (s >= 2)) + 1))


def kernel(**inputs):
    import concourse.bacc as bacc
    from concourse.bass_utils import run_bass_kernel_spmd

    a = {k.replace("L0_conv_", ""): np.asarray(v) for k, v in inputs.items()}
    r1 = C // 16

    def columns(low, high):
        m = np.zeros((96, 3), np.float32)
        m[:C, 0], m[:, 1], m[:, 2] = low, high[:96], high[96:]
        return m

    enc = a["W_enc"].transpose(1, 2, 3, 0).reshape(4 * C, TAPS * C)
    arrays = dict(
        constants(),
        x=a["x"],
        w_id=a["W_id"].transpose(1, 2, 3, 0).reshape(C, TAPS, C),
        b_id=a["b_id"].reshape(C, 1),
        wd_low=a["W_dl"].T,
        wd_high=a["W_dh"].T.reshape(C, 3, 3 * C),
        bd=columns(a["b_dl"], a["b_dh"]),
        w1_low=a["W1_low"].T,
        w1_high=a["W1_high"].T.reshape(2, 96, 3 * r1).transpose(1, 0, 2),
        w2_low=a["W2_low"].T,
        w2_high=a["W2_high"].T,
        wa_low=a["W_al"],
        wa_high=a["W_ah"].reshape(2, 96, C, 3).transpose(1, 0, 3, 2).reshape(96, 2, 3 * C),
        ba=columns(a["b_al"], a["b_ah"]),
        enc_low=enc[:C],
        enc_high=enc[C:].reshape(2, 96, TAPS * C).transpose(1, 0, 2),
        b_enc=a["b_enc"].reshape(1, C),
    )
    arrays = {f"in_{k}": np.ascontiguousarray(v) for k, v in arrays.items()}
    nc = bacc.Bacc("TRN2", target_bir_lowering=False, num_devices=1)
    tensors = {k[3:]: nc.dram_tensor(k, v.shape, mybir.dt.from_np(v.dtype), kind="ExternalInput").ap()
               for k, v in arrays.items()}
    out = nc.dram_tensor("out", (B, C, H, W), F32, kind="ExternalOutput").ap()
    conv_preact(nc, tensors, out)
    r = run_bass_kernel_spmd(nc, [arrays], core_ids=[0])
    return r.results[0]["out"]
```

```python
from contextlib import ExitStack

import numpy as np

import concourse.bass as bass
from concourse import mybir

ALU = mybir.AluOpType
ACT = mybir.ActivationFunctionType
AX = mybir.AxisListType
F32 = mybir.dt.float32
F16 = mybir.dt.float16

B, C, H, W = 8, 64, 224, 224
HW = H * W
G = 32
P = 128
HALF = H // 2
EPS = 1e-5
TAPS = 9
WP = W + 2

R = 8
NB = HALF // R
RH = R + 2
PAIRS = R // 2
NT = 2 * W
XS = 5
TURN = 4
INNER = 2
NOPEN = NB - TURN * INNER

SX = 4
OPEN_CHUNKS = [4, 5, 5, 5, 5, 4]
CPB = 6
SB = 2
SC = 9 * W // 4
CPT = CPB * SB
CPO = sum(OPEN_CHUNKS)
CPI = CPO + CPT * INNER
SC_EDGE = (HALF * W - (CPI - 8) * SC) // 8
OPEN_COLS = [SC_EDGE] * 4 + [SC] * 20 + [SC_EDGE] * 4
NREC = HALF // 2
NSTAT = CPI
assert sum(OPEN_COLS) + CPT * INNER * SC == HALF * W and CPO % SX == 0 and CPT % SX == 0

ER = 4
NE = HALF // ER
EH = ER + 2
SROWS = H + 2 + ER
CG = 8

DEC_LO = [-0.07576571478927333, -0.02963552764599851, 0.49761866763201545, 0.8037387518059161,
          0.29785779560527736, -0.09921954357684722, -0.012603967262037833, 0.0322231006040427]
DEC_HI = [-0.0322231006040427, -0.012603967262037833, 0.09921954357684722, 0.29785779560527736,
          -0.8037387518059161, 0.49761866763201545, 0.02963552764599851, -0.07576571478927333]
MX = [0, 0, 6, 0, 0, 1, 1, 4, 5, 1, 3, 0, 0, 0, 3, 2]
MY = [0, 1, 0, 5, 2, 0, 2, 0, 0, 6, 0, 4, 6, 3, 5, 2]
NK = len(MX)
NF = 7
SUM_L = float(np.sum(DEC_LO) ** 3)
SUM_H = float(np.sum(DEC_LO) ** 2 * np.sum(DEC_HI))
NG = 2 * NF
NS1 = 2 * H + NG
SUBBAND = [1, 2, 3]


def constants():
    def circulant(taps, dil):
        m = np.zeros((H, H))
        for k, f in enumerate(taps):
            for i in range(H):
                m[i, (i + k * dil) % H] += f
        return m

    level2 = circulant(DEC_LO, 2) @ circulant(DEC_LO, 1)
    low, high = circulant(DEC_LO, 4) @ level2, circulant(DEC_HI, 4) @ level2
    basis = np.zeros((NF, H))
    for u in range(NF):
        f = u * (H // 7)
        basis[u] = np.cos(np.pi * f * (np.arange(H) + 0.5) / H) / np.sqrt(H) * (np.sqrt(2.0) if f else 1.0)
    moved = np.concatenate([low.T @ basis.T, high.T @ basis.T], axis=1)
    fh = np.concatenate([low.T, high.T, moved], axis=1)
    fw = np.concatenate([low.T, high.T], axis=1)
    fw_hi = fw.astype(np.float16)
    fw_lo = (fw - fw_hi.astype(np.float64)).astype(np.float16)
    total = moved.sum(axis=0)
    of_mean = np.outer(total, total).reshape(1, NG * NG).repeat(C, axis=0)
    partner = np.zeros((P, 3, P))
    for p in range(P):
        for k, q in enumerate((p ^ 1, p ^ C, p ^ 1 ^ C)):
            partner[q, k, p] = 1.0
    pick = np.zeros((96, 3, NK))
    dsum = np.zeros((96, 3))
    bsum = basis.sum(axis=1)
    for g in range(3):
        for o in range(C if g == 0 else 96):
            k = o // (C // NK) if g == 0 else (96 * (g - 1) + o) // (3 * C // NK)
            pick[o, g, k] = 1.0
            dsum[o, g] = bsum[MX[k]] * bsum[MY[k]]
    inside = np.zeros((TAPS, H + ER, W), np.float16)
    for t in range(TAPS):
        dy, dx = t // 3 - 1, t % 3 - 1
        inside[t, max(0, -dy):H - max(0, dy), max(0, -dx):W - max(0, dx)] = 1.0
    f = np.float32
    return {
        "fh": fh.reshape(2, HALF, NS1).transpose(1, 0, 2).astype(f),
        "fw": np.stack([fw_hi, fw_lo], 1).reshape(2, HALF, 2, 2 * W).transpose(1, 0, 2, 3),
        "gw": moved.reshape(2, HALF, NG).transpose(1, 0, 2).astype(f),
        "of_mean": of_mean.astype(f),
        "partner": partner.astype(f),
        "ident": np.eye(C, dtype=f),
        "pick": pick.astype(f),
        "dsum": dsum.astype(f),
        "inside": inside.reshape(TAPS, (H + ER) * W),
    }


def conv_preact(nc, t, out):
    x = t["x"]
    scratch = nc.dram_tensor("row_filtered", (2, HALF, SROWS, 2 * P), F16, kind="Internal").ap()

    with ExitStack() as top:
        def sb(stack, name, shape, dt=F32):
            return stack.enter_context(nc.sbuf_tensor(name, shape, dt))

        def sem(stack, name):
            return stack.enter_context(nc.semaphore(name))

        psum = [top.enter_context(nc.psum_tensor(f"ps{i}", [P, 512], F32)) for i in range(8)]
        partner = sb(top, "partner", [P, 3, P])
        records = sb(top, "records", [P, NREC, 6])
        mv = sb(top, "mv", [P, 2])
        quad = sb(top, "quad", [P, 4, 2])
        gsum = sb(top, "gsum", [P, 2])
        gmean = sb(top, "gmean", [P, 1])
        dev = sb(top, "dev", [P, 4])
        dev2 = sb(top, "dev2", [P, 4])
        gvar = sb(top, "gvar", [P, 1])
        mhalf = sb(top, "mhalf", [P, 1])
        root = sb(top, "root", [P, 1])
        newt = sb(top, "newt", [P, 2])
        norm = sb(top, "norm", [P, 2])
        w_hi = sb(top, "w_hi", [P, TAPS, C], F16)
        w_lo = [sb(top, f"w_lo{s}", [P, 6, C], F16) for s in range(2)]
        w_max = sb(top, "w_max", [P, 1])
        b_id = sb(top, "b_id", [P, 1])

        def combine(dve, chain, base, ps):
            def step(n, ins):
                ins.then_inc(chain, 1)
                dve.wait_ge(chain, base + n)
            step(1, dve.tensor_copy(quad[:, 1:4, :], ps))
            step(2, dve.tensor_copy(quad[:, 0, :], mv[:, :]))
            step(3, dve.tensor_reduce(gsum[:, 0:1], quad[:, :, 0], AX.X, ALU.add))
            step(4, dve.tensor_scalar(gmean[:, :], gsum[:, 0:1], 0.25, None, ALU.mult))
            step(5, dve.tensor_scalar(dev[:, :], quad[:, :, 0], gmean[:, 0:1], None, ALU.subtract))
            step(6, dve.tensor_tensor(dev2[:, :], dev[:, :], dev[:, :], ALU.mult))
            step(7, dve.tensor_tensor(dev[:, :], dev2[:, :], quad[:, :, 1], ALU.add))
            step(8, dve.tensor_reduce(gsum[:, 1:2], dev[:, :], AX.X, ALU.add))

        def commit(dve, chain, base):
            def step(n, ins):
                ins.then_inc(chain, 1)
                dve.wait_ge(chain, base + n)
            step(1, dve.tensor_tensor(newt[:, 0:1], root[:, :], root[:, :], ALU.mult))
            step(2, dve.tensor_tensor(newt[:, 1:2], newt[:, 0:1], gvar[:, :], ALU.mult))
            step(3, dve.tensor_scalar(newt[:, 0:1], newt[:, 1:2], -0.5, 1.5, ALU.mult, ALU.add))
            step(4, dve.tensor_tensor(norm[:, 0:1], root[:, :], newt[:, 0:1], ALU.mult))
            step(5, dve.scalar_tensor_tensor(norm[:, 1:2], gmean[:, :], -1.0, norm[:, 0:1],
                                             ALU.mult, ALU.mult))

        with ExitStack() as s1:
            CR = 14
            NCH = HALF // CR
            xc = [sb(s1, f"xc{i}", [P, CR * W]) for i in range(2)]
            w32 = sb(s1, "w32", [P, TAPS, C])
            wn = sb(s1, "wn", [P, TAPS, C])
            wl = sb(s1, "wl", [P, TAPS, C], F16)
            wmx = sb(s1, "wmx", [P, 2])
            winv = sb(s1, "winv", [P, 1])
            chunk_in = [sem(s1, f"chunk_in{i}") for i in range(2)]
            consts_in = sem(s1, "consts_in")
            chunk_used = sem(s1, "chunk_used")
            aggregated = sem(s1, "aggregated")
            partners_done = sem(s1, "partners_done")
            chain1 = sem(s1, "chain1")
            mhalf_set = sem(s1, "mhalf_set")
            var_ready = sem(s1, "var_ready")
            root_ready = sem(s1, "root_ready")
            wmax_part = sem(s1, "wmax_part")
            wmax_all = sem(s1, "wmax_all")
            wchain = sem(s1, "wchain")

            with nc.Block() as block:
                @block.sync
                def _(sp):
                    sp.dma_start(partner[:, :, :], t["partner"]).then_inc(consts_in, 16)
                    for s in range(2):
                        sp.dma_start(w32[C * s:C * s + C, :, :], t["w_id"]).then_inc(consts_in, 16)
                        sp.dma_start(b_id[C * s:C * s + C, :], t["b_id"]).then_inc(consts_in, 16)
                    with sp.Fori(0, NCH // 2) as i:
                        for n in range(2):
                            sp.wait_ge(chunk_used, 2 * i + n + 1)
                            for s in range(2):
                                src = x[0, :, bass.ds(s * HALF + (2 * i + n) * CR, CR), :]
                                sp.dma_start(xc[n][C * s:C * s + C, :],
                                             src.rearrange("c h w -> c (h w)")).then_inc(chunk_in[n], 16)

                @block.vector
                def _(dve):
                    def step(n, ins):
                        ins.then_inc(wchain, 1)
                        dve.wait_ge(wchain, n)
                    dve.memset(mhalf[:, :], -0.5).then_inc(mhalf_set, 1)
                    dve.memset(winv[:, :], 0.0).then_inc(chunk_used, 2)
                    dve.wait_ge(chunk_used, 2)
                    for s in range(2):
                        dve.memset(w_lo[s][:, :, :], 0.0).then_inc(mhalf_set, 1)
                    dve.wait_ge(mhalf_set, 3)
                    dve.wait_ge(consts_in, 80)
                    dve.tensor_reduce(wmx[:, 0:1], w32[:, :, :].rearrange("p a b -> p (a b)"), AX.X, ALU.max,
                                      apply_absolute_value=True).then_inc(wmax_part, 1)
                    dve.wait_ge(wmax_all, 1)
                    step(1, dve.tensor_scalar(w_max[:, :], wmx[:, 1:2], 1e-30, None, ALU.max))
                    step(2, dve.reciprocal(winv[:, :], w_max[:, :]))
                    step(3, dve.tensor_scalar(wn[:, :, :], w32[:, :, :], winv[:, 0:1], None, ALU.mult))
                    step(4, dve.tensor_copy(w_hi[:, :, :], wn[:, :, :]))
                    step(5, dve.tensor_tensor(wl[:, :, :], wn[:, :, :], w_hi[:, :, :], ALU.subtract))
                    own, other = slice(0, 3), slice(3, 6)
                    step(6, dve.tensor_copy(w_lo[0][0:C, 0:3, :], wl[0:C, own, :]))
                    step(7, dve.tensor_copy(w_lo[0][C:P, 0:3, :], wl[C:P, other, :]))
                    step(8, dve.tensor_copy(w_lo[0][C:P, 3:6, :], wl[C:P, 6:9, :]))
                    step(9, dve.tensor_copy(w_lo[1][C:P, 0:3, :], wl[C:P, own, :]))
                    step(10, dve.tensor_copy(w_lo[1][0:C, 0:3, :], wl[0:C, other, :]))
                    step(11, dve.tensor_copy(w_lo[1][0:C, 3:6, :], wl[0:C, 6:9, :]))
                    per = CR // 2
                    with dve.Fori(0, NCH // 2) as i:
                        for n in range(2):
                            dve.wait_ge(chunk_in[n], 32 * i + 32)
                            for k in range(per):
                                ins = dve.bn_stats(
                                    records[:, bass.ds((2 * i + n) * per + k, 1), :].rearrange("p a b -> p (a b)"),
                                    xc[n][:, k * NT:k * NT + NT])
                            ins.then_inc(chunk_used, 1)
                    dve.wait_ge(chunk_used, NCH + 2)
                    dve.bn_aggr(mv[:, :], records[:, :, :].rearrange("p a b -> p (a b)")).then_inc(aggregated, 1)
                    dve.wait_ge(partners_done, 1)
                    combine(dve, chain1, 0, psum[7][:, 0:6].rearrange("p (a b) -> p a b", a=3))
                    dve.tensor_scalar(gvar[:, :], gsum[:, 1:2], 0.25, EPS, ALU.mult, ALU.add).then_inc(var_ready, 1)
                    dve.wait_ge(root_ready, 1)
                    commit(dve, chain1, 8)

                @block.tensor
                def _(pe):
                    pe.wait_ge(consts_in, 80)
                    pe.wait_ge(aggregated, 1)
                    for k in range(3):
                        mm = pe.matmul(psum[7][:, 2 * k:2 * k + 2], partner[:, k, :], mv[:, :], start=True, stop=True)
                    mm.then_inc(partners_done, 1)

                @block.gpsimd
                def _(pool):
                    pool.wait_ge(wmax_part, 1)
                    pool.partition_all_reduce(wmx[:, 1:2], wmx[:, 0:1], P, bass.bass_isa.ReduceOp.max).then_inc(wmax_all, 1)
                    pool.wait_ge(mhalf_set, 1)
                    pool.wait_ge(var_ready, 1)
                    pool.tensor_tensor(root[:, :], gvar[:, :], mhalf[:, :], ALU.pow).then_inc(root_ready, 1)

        shared = [sb(top, f"shared{k}", [P, TAPS * C]) for k in range(2)]
        weff = [m[:, :].bitcast(F16).rearrange("p (s t e) -> p s t e", s=2, t=TAPS) for m in shared]
        bw = [sb(top, f"bw{k}", [P, C], F16) for k in range(2)]
        e_max = sb(top, "e_max", [P, 1])
        with ExitStack() as pre:
            fh = sb(pre, "fh", [HALF, 2, NS1])
            u_sum = sb(pre, "u_sum", [HALF, 2, C, NG])
            norm_row = sb(pre, "norm_row", [P, 3, C])

            with ExitStack() as s2:
                xg = [sb(s2, f"xg{i}", [HALF, 2, CG, HALF]) for i in range(2)]
                rows = sb(s2, "rows", [HALF, H, 2, 2, C], F16)
                tmp = sb(s2, "tmp", [HALF, 4, 2 * H])
                ones = sb(s2, "ones", [C, P])
                ident = sb(s2, "ident", [C, C])
                diag = sb(s2, "diag", [C, 2, C])
                zrow = sb(s2, "zrow", [HALF, 2 * P * (SROWS - H - 1)], F16)
                fh_in = sem(s2, "fh_in")
                diag_ready = sem(s2, "diag_ready")
                spread_done = sem(s2, "spread_done")
                row_ready = sem(s2, "row_ready")
                zrow_ready = sem(s2, "zrow_ready")
                group_in = [sem(s2, f"group_in{i}") for i in range(2)]
                product = sem(s2, "product")
                scaled = sem(s2, "scaled")
                hi_made = sem(s2, "hi_made")
                split = sem(s2, "split")
                rows_out = sem(s2, "rows_out")
                zeros_out = sem(s2, "zeros_out")
                NGR = C // CG

                with nc.Block() as block:
                    @block.sync
                    def _(sp):
                        sp.dma_start(fh[:, :, :], t["fh"]).then_inc(fh_in, 16)
                        sp.dma_start(ident[:, :], t["ident"]).then_inc(fh_in, 16)
                        sp.wait_ge(zrow_ready, 1)
                        for wc in range(2):
                            sp.dma_start(scratch[wc, :, 0, :], zrow[:, 0:2 * P]).then_inc(zeros_out, 16)
                            sp.dma_start(scratch[wc, :, H + 1:SROWS, :].rearrange("w r e -> w (r e)"),
                                         zrow[:, :]).then_inc(zeros_out, 16)
                        for k in range(2 * NGR):
                            wc, g = k // NGR, k % NGR
                            if k >= 2:
                                sp.wait_ge(product, CG * (k - 1))
                            for hc in range(2):
                                src = x[0, g * CG:g * CG + CG, hc * HALF:hc * HALF + HALF, wc * HALF:wc * HALF + HALF]
                                sp.dma_start(xg[k % 2][:, hc, :, :], src.rearrange("c h w -> h c w"))\
                                  .then_inc(group_in[k % 2], 16)
                        sp.wait_ge(zeros_out, 64)

                    @block.tensor
                    def _(pe):
                        pe.wait_ge(diag_ready, 3)
                        pe.matmul(psum[7][:, 0:2 * C], ones[:, :], diag[:, :, :].rearrange("p a b -> p (a b)"),
                                  start=True, stop=True).then_inc(spread_done, 1)
                        pe.wait_ge(fh_in, 32)
                        pe.wait_ge(row_ready, 3)
                        for wc in range(2):
                            with pe.Fori(0, NGR // 2) as i:
                                for n in range(2):
                                    g = wc * NGR + 2 * i + n
                                    pe.wait_ge(group_in[n], 32 * (wc * (NGR // 2) + i) + 32)
                                    for c in range(CG):
                                        pe.wait_ge(scaled, CG * g + c + 1)
                                        for hc in range(2):
                                            mm = pe.matmul(psum[c][0:HALF, 0:NS1], xg[n][:, hc, c, :], fh[:, hc, :],
                                                           start=(hc == 0), stop=(hc == 1))
                                        mm.then_inc(product, 1)

                    @block.scalar
                    def _(act):
                        act.wait_ge(row_ready, 3)
                        for wc in range(2):
                            with act.Fori(0, NGR // 2) as i:
                                for n in range(2):
                                    g = wc * NGR + 2 * i + n
                                    for c in range(CG):
                                        act.wait_ge(product, CG * g + c + 1)
                                        act.wait_ge(split, CG * g + c + 1)
                                        ch = bass.ds((2 * i + n) * CG + c, 1)
                                        for p in range(2):
                                            act.activation(tmp[:, c % 4, p * H:p * H + H], psum[c][0:HALF, p * H:p * H + H],
                                                           ACT.Identity, scale=norm_row[0:HALF, 0, ch],
                                                           bias=norm_row[0:HALF, 1 + p, ch])
                                        act.activation(
                                            u_sum[:, wc, ch, :].rearrange("p a b -> p (a b)"), psum[c][0:HALF, 2 * H:NS1],
                                            ACT.Identity).then_inc(scaled, 1)

                    @block.vector
                    def _(dve):
                        dve.memset(zrow[:, :], 0.0).then_inc(zrow_ready, 1)
                        dve.memset(diag[:, 0, 0:1], 0.0).then_inc(scaled, CG)
                        dve.memset(diag[:, 1, 0:1], 0.0).then_inc(split, 4)
                        dve.wait_ge(scaled, CG)
                        dve.wait_ge(split, 4)
                        dve.memset(ones[:, :], 1.0).then_inc(diag_ready, 1)
                        dve.wait_ge(fh_in, 32)
                        for k in range(2):
                            dve.tensor_scalar(diag[:, k, :], ident[:, :], norm[0:C, k:k + 1], None, ALU.mult)\
                               .then_inc(diag_ready, 1)
                        dve.wait_ge(spread_done, 1)
                        dve.tensor_copy(norm_row[:, 0, :], psum[7][:, 0:C]).then_inc(row_ready, 1)
                        dve.tensor_scalar(norm_row[:, 1, :], psum[7][:, C:2 * C], SUM_L, None, ALU.mult).then_inc(row_ready, 1)
                        dve.tensor_scalar(norm_row[:, 2, :], psum[7][:, C:2 * C], SUM_H, None, ALU.mult).then_inc(row_ready, 1)
                        for wc in range(2):
                            if wc:
                                dve.wait_ge(rows_out, 16)
                            with dve.Fori(0, NGR // 2) as i:
                                for n in range(2):
                                    g = wc * NGR + 2 * i + n
                                    for c in range(CG):
                                        dve.wait_ge(scaled, CG * g + c + 1 + CG)
                                        ch = bass.ds((2 * i + n) * CG + c, 1)
                                        v = tmp[:, c % 4, :].rearrange("w (p r) -> w r p", p=2)
                                        hi = rows[:, :, 0, :, ch].rearrange("w r p a -> w r (p a)")
                                        lo = rows[:, :, 1, :, ch].rearrange("w r p a -> w r (p a)")
                                        dve.tensor_copy(hi, v).then_inc(hi_made, 1)
                                        dve.wait_ge(hi_made, CG * g + c + 1)
                                        dve.tensor_tensor(lo, v, hi, ALU.subtract).then_inc(split, 1)

                    @block.gpsimd
                    def _(pool):
                        for wc in range(2):
                            pool.wait_ge(split, C * (wc + 1) + 4)
                            pool.dma_start(scratch[wc, :, 1:H + 1, :].rearrange("w r e -> w (r e)"),
                                           rows[:, :, :, :, :].rearrange("w r k p c -> w (r k p c)")).then_inc(rows_out, 16)
                        pool.wait_ge(rows_out, 32)

            with ExitStack() as s3:
                names = ["gw", "of_mean", "pick", "dsum", "wd_low", "wd_high", "bd", "w1_low", "w1_high",
                         "w2_low", "w2_high", "wa_low", "wa_high", "ba", "enc_low", "enc_high", "b_enc"]
                c3 = {n: sb(s3, n, list(t[n].shape)) for n in names}
                tn = sb(s3, "tn", [C, NG * NG])
                tc = sb(s3, "tc", [C, NG * NG])
                sk = sb(s3, "sk", [C, 4, NK])
                neg_m = sb(s3, "neg_m", [P, 1])
                junk = sb(s3, "junk", [96, 3, NK])
                yd = sb(s3, "yd", [96, 3])
                yb = sb(s3, "yb", [96, 3])
                y = sb(s3, "y", [96, 3])
                z = sb(s3, "z", [12, 2])
                sg = sb(s3, "sg", [96, 3])
                bs = sb(s3, "bs", [96, 3])
                was_low = sb(s3, "was_low", [C, C])
                was_high = sb(s3, "was_high", [96, 2, 3 * C])
                e32 = sb(s3, "e32", [P, 2, TAPS * C])
                en = sb(s3, "en", [P, 2, TAPS * C])
                brow = sb(s3, "brow", [1, TAPS * C])
                b32 = sb(s3, "b32", [P, C])
                bn = sb(s3, "bn", [P, C])
                emx = sb(s3, "emx", [P, 4])
                einv = sb(s3, "einv", [P, 1])
                in3 = sem(s3, "in3")
                dch = sem(s3, "dch")
                t_done = sem(s3, "t_done")
                s_ready = sem(s3, "s_ready")
                y_done = sem(s3, "y_done")
                y_ready = sem(s3, "y_ready")
                z_done = sem(s3, "z_done")
                z_ready = sem(s3, "z_ready")
                sc_done = sem(s3, "sc_done")
                sig_done = sem(s3, "sig_done")
                was_ready = sem(s3, "was_ready")
                e_done = sem(s3, "e_done")
                brow_ready = sem(s3, "brow_ready")
                b32_in = sem(s3, "b32_in")
                emax_part = sem(s3, "emax_part")
                emax_all = sem(s3, "emax_all")
                HN = TAPS * C // 2

                with nc.Block() as block:
                    @block.sync
                    def _(sp):
                        for n in names:
                            sp.dma_start(c3[n][(slice(None),) * len(t[n].shape)], t[n]).then_inc(in3, 16)
                        sp.wait_ge(brow_ready, 2)
                        sp.dma_start(b32[0:TAPS, :], brow[0:1, :].rearrange("a (t e) -> a t e", t=TAPS)).then_inc(b32_in, 16)

                    @block.tensor
                    def _(pe):
                        pe.wait_ge(in3, 16 * len(names))
                        for u in range(NG):
                            for wc in range(2):
                                mm = pe.matmul(psum[0][0:C, u * NG:u * NG + NG], u_sum[:, wc, :, u], c3["gw"][:, wc, :],
                                               start=(wc == 0), stop=(wc == 1))
                        mm.then_inc(t_done, 1)
                        pe.wait_ge(s_ready, 1)
                        pe.matmul(psum[1][0:C, 0:NK], c3["wd_low"][:, :], sk[:, 0, :], start=True, stop=True)
                        for g in range(2):
                            for j in range(3):
                                mm = pe.matmul(psum[1][0:96, NK * (1 + g):NK * (2 + g)],
                                               c3["wd_high"][:, j, 96 * g:96 * g + 96], sk[:, SUBBAND[j], :],
                                               start=(j == 0), stop=(j == 2))
                        mm.then_inc(y_done, 1)
                        pe.wait_ge(y_ready, 1)
                        pe.matmul(psum[2][0:4, 0:1], c3["w1_low"][:, :], y[0:C, 0:1], start=True, stop=True)
                        for g in range(2):
                            mm = pe.matmul(psum[2][0:12, 1:2], c3["w1_high"][:, g, :], y[:, 1 + g:2 + g],
                                           start=(g == 0), stop=(g == 1))
                        mm.then_inc(z_done, 1)
                        pe.wait_ge(z_ready, 2)
                        pe.matmul(psum[3][0:C, 0:1], c3["w2_low"][:, :], z[0:4, 0:1], start=True, stop=True)
                        for g in range(2):
                            mm = pe.matmul(psum[3][0:96, 1 + g:2 + g], c3["w2_high"][:, 96 * g:96 * g + 96], z[0:12, 1:2],
                                           start=True, stop=True)
                        mm.then_inc(sc_done, 1)
                        pe.wait_ge(was_ready, 6)
                        for sw in range(2):
                            for n in range(2):
                                ps = psum[4 + 2 * sw + n]
                                cols = slice(n * HN, n * HN + HN)
                                for sh in range(2):
                                    o = ps[C * sh:C * sh + C, 0:HN]
                                    sub = 2 * sh + sw
                                    if sub == 0:
                                        pe.matmul(o, was_low[:, :], c3["enc_low"][:, cols], start=True, stop=True)
                                        continue
                                    for g in range(2):
                                        pe.matmul(o, was_high[:, g, C * (sub - 1):C * sub], c3["enc_high"][:, g, cols],
                                                  start=(g == 0), stop=(g == 1))
                        for n in range(2):
                            cols = slice(n * HN, n * HN + HN)
                            o = psum[n][0:1, 0:HN]
                            pe.matmul(o, bs[0:C, 0:1], c3["enc_low"][:, cols], start=True, stop=False)
                            for g in range(2):
                                mm = pe.matmul(o, bs[:, 1 + g:2 + g], c3["enc_high"][:, g, cols], start=False, stop=(g == 1))
                        mm.then_inc(e_done, 1)

                    @block.scalar
                    def _(act):
                        act.wait_ge(sc_done, 1)
                        act.activation(sg[0:C, 0:1], psum[3][0:C, 0:1], ACT.Sigmoid).then_inc(sig_done, 1)
                        act.activation(sg[:, 1:3], psum[3][0:96, 1:3], ACT.Sigmoid).then_inc(sig_done, 1)

                    @block.vector
                    def _(dve):
                        count = [0]

                        def step(ins):
                            count[0] += 1
                            ins.then_inc(dch, 1)
                            dve.wait_ge(dch, count[0])
                        step(dve.memset(yd[:, :], 0.0))
                        step(dve.memset(b32[:, :], 0.0))
                        dve.wait_ge(in3, 16 * len(names))
                        step(dve.tensor_scalar(neg_m[:, :], gmean[:, :], -1.0, None, ALU.mult))
                        dve.wait_ge(t_done, 1)
                        step(dve.scalar_tensor_tensor(tc[:, :], c3["of_mean"][:, :], neg_m[0:C, 0:1], psum[0][0:C, 0:NG * NG],
                                                      ALU.mult, ALU.add))
                        step(dve.tensor_scalar(tn[:, :], tc[:, :], norm[0:C, 0:1], None, ALU.mult))
                        tv = tn[:, :].rearrange("c (a u b v) -> c a u b v", a=2, u=NF, b=2)
                        so = sk[:, :, :].rearrange("c (a b) k -> c a b k", a=2)
                        for k in range(NK):
                            ins = dve.tensor_copy(so[:, :, :, k], tv[:, :, MX[k], :, MY[k]])
                        count[0] += 1
                        ins.then_inc(dch, 1)
                        dve.wait_ge(dch, count[0])
                        dve.tensor_tensor(yb[:, :], c3["bd"][:, :], c3["dsum"][:, :], ALU.mult).then_inc(s_ready, 1)
                        dve.wait_ge(s_ready, 1)
                        dve.wait_ge(y_done, 1)
                        for g in range(3):
                            m = C if g == 0 else 96
                            step(dve.tensor_tensor_reduce(junk[0:m, g, :], psum[1][0:m, NK * g:NK * g + NK],
                                                          c3["pick"][0:m, g, :], 1.0, 0.0, ALU.mult, ALU.add,
                                                          yd[0:m, g:g + 1]))
                        dve.tensor_tensor(y[:, :], yd[:, :], yb[:, :], ALU.add).then_inc(y_ready, 1)
                        dve.wait_ge(z_done, 1)
                        dve.tensor_scalar(z[0:4, 0:1], psum[2][0:4, 0:1], 0.0, None, ALU.max).then_inc(z_ready, 1)
                        dve.tensor_scalar(z[0:12, 1:2], psum[2][0:12, 1:2], 0.0, None, ALU.max).then_inc(z_ready, 1)
                        dve.wait_ge(sig_done, 2)
                        dve.tensor_scalar(was_low[:, :], c3["wa_low"][:, :], sg[0:C, 0:1], None, ALU.mult).then_inc(was_ready, 1)
                        for g in range(2):
                            dve.tensor_scalar(was_high[:, g, :], c3["wa_high"][:, g, :], sg[:, 1 + g:2 + g], None, ALU.mult)\
                               .then_inc(was_ready, 1)
                        dve.tensor_tensor(bs[0:C, 0:1], c3["ba"][0:C, 0:1], sg[0:C, 0:1], ALU.mult).then_inc(was_ready, 1)
                        dve.tensor_tensor(bs[:, 1:3], c3["ba"][:, 1:3], sg[:, 1:3], ALU.mult).then_inc(was_ready, 1)
                        dve.memset(emx[:, :], 0.0).then_inc(was_ready, 1)
                        dve.wait_ge(e_done, 1)
                        for sw in range(2):
                            for n in range(2):
                                ins = dve.tensor_copy(e32[:, sw, n * HN:n * HN + HN], psum[4 + 2 * sw + n][:, 0:HN])
                        step(ins)
                        dve.tensor_copy(brow[0:1, 0:HN], psum[0][0:1, 0:HN]).then_inc(brow_ready, 1)
                        step(dve.tensor_copy(brow[0:1, HN:2 * HN], psum[1][0:1, 0:HN]))
                        mid = slice(4 * C, 5 * C)
                        dve.wait_ge(brow_ready, 1)
                        dve.tensor_tensor(brow[0:1, mid], brow[0:1, mid], c3["b_enc"][0:1, :], ALU.add).then_inc(brow_ready, 1)
                        dve.wait_ge(b32_in, 16)
                        dve.wait_ge(was_ready, 6)
                        step(dve.tensor_reduce(emx[:, 0:1], e32[:, :, :].rearrange("p a b -> p (a b)"), AX.X, ALU.max,
                                               apply_absolute_value=True))
                        step(dve.tensor_reduce(emx[:, 1:2], b32[:, :], AX.X, ALU.max, apply_absolute_value=True))
                        dve.tensor_reduce(emx[:, 2:3], emx[:, 0:2], AX.X, ALU.max).then_inc(emax_part, 1)
                        dve.wait_ge(emax_all, 1)
                        step(dve.tensor_scalar(e_max[:, :], emx[:, 3:4], 1e-30, None, ALU.max))
                        step(dve.reciprocal(einv[:, :], e_max[:, :]))
                        step(dve.tensor_scalar(en[:, :, :], e32[:, :, :], einv[:, 0:1], None, ALU.mult))
                        step(dve.tensor_scalar(bn[:, :], b32[:, :], einv[:, 0:1], None, ALU.mult))
                        ev = en[:, :, :].rearrange("p s (t e) -> p (s t) e", t=TAPS)
                        wv = [w[:, :, :, :].rearrange("p s t e -> p (s t) e") for w in weff]
                        step(dve.tensor_copy(wv[0], ev))
                        step(dve.tensor_copy(bw[0][:, :], bn[:, :]))
                        step(dve.tensor_tensor(wv[1], ev, wv[0], ALU.subtract))
                        step(dve.tensor_tensor(bw[1][:, :], bn[:, :], bw[0][:, :], ALU.subtract))

                    @block.gpsimd
                    def _(pool):
                        pool.wait_ge(emax_part, 1)
                        pool.partition_all_reduce(emx[:, 3:4], emx[:, 2:3], P, bass.bass_isa.ReduceOp.max)\
                            .then_inc(emax_all, 1)

        e_map = sb(top, "e_map", [P, HALF * W])
        encoder(nc, t, scratch, psum, sb, sem, weff, bw, e_max, b_id, e_map)
        main(nc, x, shared, out, psum, sb, sem, e_map, partner, records, mv, quad, dev2, gsum, gvar, mhalf, root, norm, newt,
             w_hi, w_lo, w_max, combine, commit)


def encoder(nc, t, scratch, psum, sb, sem, weff, bw, e_max, b_id, e_map):
    with ExitStack() as s4:
        fw = sb(s4, "fw", [HALF, 2, 2, 2 * W], F16)
        s_in = [sb(s4, f"s_in{i}", [HALF, 2, 2, ER, 2 * P], F16) for i in range(2)]
        s_halo = sb(s4, "s_halo", [HALF, 2, 2, 2, 2 * P], F16)
        d = [sb(s4, f"d{i}", [P, 4, EH, 2, WP], F16) for i in range(2)]
        inside = [sb(s4, f"inside{i}", [P, 2, ER * W], F16) for i in range(2)]
        lin = sb(s4, "lin", [P, 2, NT])
        leak = sb(s4, "leak", [P, 2, NT])
        fw_in = sem(s4, "fw_in")
        halo_in = sem(s4, "halo_in")
        step_in = [sem(s4, f"step_in{i}") for i in range(2)]
        inside_in = [sem(s4, f"inside_in{i}") for i in range(2)]
        pads_set = sem(s4, "pads_set")
        gen_done = sem(s4, "gen_done")
        hi_done = sem(s4, "hi_done")
        lo_done = sem(s4, "lo_done")
        carried = sem(s4, "carried")
        conv_done = sem(s4, "conv_done")
        lin_done = sem(s4, "lin_done")
        leak_done = sem(s4, "leak_done")
        map_done = sem(s4, "map_done")
        FIRST = 2 * EH

        with nc.Block() as block:
            @block.sync
            def _(sp):
                def load(buf, row0, n, signal):
                    for wc in range(2):
                        for s in range(2):
                            sp.dma_start(buf[:, wc, s, :, :].rearrange("w r e -> w (r e)"),
                                         scratch[wc, :, bass.ds(row0 + HALF * s, n), :].rearrange("w r e -> w (r e)"))\
                              .then_inc(signal, 16)
                sp.dma_start(fw[:, :, :, :], t["fw"]).then_inc(fw_in, 16)
                load(s_halo, 0, 2, halo_in)
                load(s_in[0], 2, ER, step_in[0])
                def load_inside(n, step):
                    for s in range(2):
                        sp.dma_start(inside[n][0:TAPS, s, :], t["inside"][:, bass.ds((ER * step + HALF * s) * W, ER * W)])\
                          .then_inc(inside_in[n], 16)
                sp.wait_ge(pads_set, 6)
                load_inside(0, 0)
                with sp.Fori(0, NE // 2) as i:
                    for n in range(2):
                        step = 2 * i + n
                        m = (n + 1) % 2
                        sp.wait_ge(gen_done, FIRST + 8 * step)
                        load(s_in[m], ER * (step + 1) + 2, ER, step_in[m])
                        sp.wait_ge(conv_done, 2 * step + 1)
                        load_inside(m, step + 1)
                sp.wait_ge(inside_in[0], 32 * (NE // 2 + 1))

            @block.tensor
            def _(pe):
                def gen(tile, lhs):
                    k = 0
                    for wc in range(2):
                        for a, b in ((0, 0), (0, 1), (1, 0)):
                            mm = pe.matmul(psum[tile % 4][:, 0:NT], lhs[:, wc, P * a:P * a + P], fw[:, wc, b, :],
                                           start=(k == 0), stop=(k == 5))
                            k += 1
                    mm.then_inc(gen_done, 1)

                def conv(step, n, q):
                    o = psum[4 + 2 * n + q]
                    pieces = [(weff[a][:, sw, 3 * ky + kx, :], b, ky, kx, sw)
                              for a, b in ((0, 0), (0, 1), (1, 0)) for sw in range(2) for ky in range(3) for kx in range(3)]
                    for k, (w, b, ky, kx, sw) in enumerate(pieces):
                        for s in range(2):
                            pe.matmul(o[C * s:C * s + C, 0:NT], w,
                                      d[n][:, 2 * s + b, 2 * q + ky:2 * q + ky + 2, sw, kx:kx + W], start=(k == 0), stop=False)
                    for a in range(2):
                        for s in range(2):
                            mm = pe.matmul(o[C * s:C * s + C, 0:NT], bw[a][:, :],
                                           inside[n][:, s, 2 * q * W:2 * q * W + NT], start=False, stop=(a == 1))
                    mm.then_inc(conv_done, 1)

                pe.wait_ge(fw_in, 16)
                pe.wait_ge(halo_in, 64)
                pe.wait_ge(step_in[0], 64)
                pe.wait_ge(pads_set, 6)
                for k in range(FIRST):
                    if k >= 4:
                        pe.wait_ge(lo_done, k - 3)
                    s, r = k % 2, k // 2
                    gen(k, s_halo[:, :, s, r, :] if r < 2 else s_in[0][:, :, s, r - 2, :])
                with pe.Fori(0, NE // 2) as i:
                    for n in range(2):
                        step = 2 * i + n
                        m = (n + 1) % 2
                        pe.wait_ge(step_in[m], 64 * (i + 1) + (0 if n == 0 else 64))
                        for k in range(8):
                            pe.wait_ge(lo_done, FIRST + 8 * step + k - 3)
                            gen(k, s_in[m][:, :, k % 2, k // 2, :])
                        pe.wait_ge(lo_done, FIRST + 8 * step)
                        pe.wait_ge(carried, step + 1)
                        pe.wait_ge(inside_in[n], 32 * i + 32)
                        pe.wait_ge(leak_done, 2 * step + 1)
                        for q in range(2):
                            conv(step, n, q)

            @block.scalar
            def _(act):
                def hi(tile, k, slot, s, r):
                    act.wait_ge(gen_done, tile + 1)
                    act.copy(d[slot][:, 2 * s, r, :, 1:1 + W], psum[k % 4][:, 0:NT].rearrange("p (a w) -> p a w", a=2))\
                       .then_inc(hi_done, 1)

                act.wait_ge(pads_set, 6)
                for k in range(FIRST):
                    hi(k, k, 0, k % 2, k // 2)
                with act.Fori(0, NE // 2) as i:
                    for n in range(2):
                        step = 2 * i + n
                        m = (n + 1) % 2
                        act.wait_ge(conv_done, 2 * step + 1)
                        for k in range(8):
                            hi(FIRST + 8 * step + k, k, m, k % 2, 2 + k // 2)
                        for q in range(2):
                            act.wait_ge(conv_done, 2 * step + q + 2)
                            act.wait_ge(leak_done, 2 * step + q + 1)
                            act.activation(lin[:, q, :], psum[4 + 2 * n + q][:, 0:NT], ACT.Identity, scale=e_max[:, 0:1])\
                               .then_inc(lin_done, 1)

            @block.vector
            def _(dve):
                def lo(tile, k, slot, s, r):
                    dve.wait_ge(hi_done, tile + 1)
                    dve.tensor_tensor(d[slot][:, 2 * s + 1, r, :, 1:1 + W], psum[k % 4][:, 0:NT].rearrange("p (a w) -> p a w", a=2),
                                      d[slot][:, 2 * s, r, :, 1:1 + W], ALU.subtract).then_inc(lo_done, 1)

                for n in range(2):
                    dv = d[n][:, :, :, :, :].rearrange("p a r s w -> p (a r s) w")
                    dve.memset(dv[:, :, 0:1], 0.0).then_inc(pads_set, 1)
                    dve.memset(dv[:, :, WP - 1:WP], 0.0).then_inc(pads_set, 1)
                    dve.memset(inside[n][:, :, :], 0.0).then_inc(pads_set, 1)
                for k, counter in enumerate((conv_done, carried, leak_done, map_done)):
                    dve.memset(leak[:, 0, k:k + 1], 0.0).then_inc(counter, 1)
                dve.wait_ge(pads_set, 6)
                dve.wait_ge(leak_done, 1)
                dve.wait_ge(map_done, 1)
                dve.wait_ge(fw_in, 16)
                for k in range(FIRST):
                    lo(k, k, 0, k % 2, k // 2)
                with dve.Fori(0, NE // 2) as i:
                    for n in range(2):
                        step = 2 * i + n
                        m = (n + 1) % 2
                        dve.wait_ge(conv_done, 2 * step + 1)
                        dve.wait_ge(lo_done, FIRST + 8 * step)
                        dve.tensor_copy(d[m][:, :, 0:2, :, :].rearrange("p a r s w -> p a (r s w)"),
                                        d[n][:, :, ER:EH, :, :].rearrange("p a r s w -> p a (r s w)")).then_inc(carried, 1)
                        for k in range(8):
                            lo(FIRST + 8 * step + k, k, m, k % 2, 2 + k // 2)
                        for q in range(2):
                            dve.wait_ge(lin_done, 2 * step + q + 1)
                            dve.wait_ge(map_done, 2 * step + q + 1)
                            dve.scalar_tensor_tensor(leak[:, q, :], lin[:, q, :], 0.01, lin[:, q, :], ALU.mult, ALU.max)\
                               .then_inc(leak_done, 1)
                            dve.wait_ge(leak_done, 2 * step + q + 2)
                            dve.tensor_scalar(e_map[:, bass.ds((ER * step + 2 * q) * W, NT)], leak[:, q, :], b_id[:, 0:1], None,
                                              ALU.add).then_inc(map_done, 1)


def main(nc, x, shared, out, psum, sb, sem, e_map, partner, records, mv, quad, dev2, gsum, gvar, mhalf, root, norm, newt,
         w_hi, w_lo, w_max, combine, commit):
    with ExitStack() as s5:
        xs = [sb(s5, f"xs{i}", [P, RH * W]) for i in range(XS)]
        xn = sb(s5, "xn", [P, RH * W])
        norm_now = sb(s5, "norm_now", [P, 2])
        same = [[sb(s5, f"same{i}{s}", [P, RH, WP], F16) for s in range(2)] for i in range(2)]
        next_ = [[sb(s5, f"next{i}{s}", [P, RH - 1, WP], F16) for s in range(2)] for i in range(2)]
        stage = sb(s5, "stage", [P, PAIRS, NT])
        sx = [sb(s5, f"sx{i}", [P, SC]) for i in range(SX - 2)] + shared

        x_in = [sem(s5, f"x_in{i}") for i in range(XS)]
        x_free = [sem(s5, f"x_free{i}") for i in range(XS)]
        stat_in = [sem(s5, f"stat_in{i}") for i in range(SX)]
        stat_used = sem(s5, "stat_used")
        tiles = sem(s5, "tiles")
        act_prep = sem(s5, "act_prep")
        dve_prep = sem(s5, "dve_prep")
        split_edge = sem(s5, "split_edge")
        evac = sem(s5, "evac")
        added = sem(s5, "added")
        normed = sem(s5, "normed")
        norm_taken = sem(s5, "norm_taken")
        chain = sem(s5, "chain")
        commits = sem(s5, "commits")
        aggregated = sem(s5, "aggregated5")
        partners_done = sem(s5, "partners_done5")
        var_ready = sem(s5, "var_ready5")
        root_ready = sem(s5, "root_ready5")
        TOP, BOTTOM, IN = range(3)

        def opening(i):
            n = NB * i
            return ([(n, 0, 4, 2 * i, BOTTOM, NB - 1)]
                    + [(n + 1 + j, (1 + j) % 2, j, (1 + INNER) * i, IN, NB - 1 - TURN + j) for j in range(TURN)]
                    + [(n + 5, 1, 4, 2 * i + 1, TOP, 0)])

        def inner(i, it, j):
            return NB * i + NOPEN + TURN * it + j, j % 2, j, (1 + INNER) * i + 1 + it, IN, 1 + TURN * it + j

        def opening_chunks(k):
            first = sum(OPEN_CHUNKS[:k])
            return list(range(first, first + OPEN_CHUNKS[k]))

        with nc.Block() as block:
            @block.sync
            def _(sp):
                def load(i, n, p, slot, u, kind, band):
                    top_row = band * R if isinstance(band, int) else sp.snap(band * R)
                    sp.wait_ge(x_free[slot], 32 * u + 32)
                    for s in (1, 0):
                        lo_row, hi_row = 0, RH
                        if kind == TOP and s == 0:
                            lo_row = 1
                        if kind == BOTTOM and s == 1:
                            hi_row = RH - 1
                        rows = hi_row - lo_row
                        src = x[bass.ds(i, 1), :, bass.ds(HALF * s + top_row - 1 + lo_row, rows), :]
                        sp.dma_start(xs[slot][C * s:C * s + C, lo_row * W:hi_row * W],
                                     src.rearrange("a c h w -> (a c) (h w)")).then_inc(x_in[slot], 16)

                def load_stats(nxt, k, m, col0, cols):
                    sp.wait_ge(stat_used, k + 1)
                    for s in range(2):
                        src = x[bass.ds(nxt, 1), :, HALF * s:HALF * s + HALF, :].rearrange("a c h w -> (a c) (h w)")
                        sp.dma_start(sx[m][C * s:C * s + C, 0:cols], src[:, bass.ds(col0, cols)]).then_inc(stat_in[m], 16)

                with sp.Fori(0, B) as i:
                    nxt = sp.snap((i + 1) % B)
                    bands = opening(i)
                    load(i, *bands[0])
                    for k in range(NOPEN):
                        if k + 1 < NOPEN:
                            load(i, *bands[k + 1])
                        for c in opening_chunks(k):
                            load_stats(nxt, CPI * i + c, c % SX, sum(OPEN_COLS[:c]), OPEN_COLS[c])
                    with sp.Fori(0, INNER) as it:
                        load(i, *inner(i, it, 0))
                        for j in range(TURN):
                            if j + 1 < TURN:
                                load(i, *inner(i, it, j + 1))
                            for c in range(CPB * j, CPB * j + CPB) if j < SB else ():
                                load_stats(nxt, CPI * i + CPO + CPT * it + c, c % SX, sum(OPEN_COLS) + SC * (CPT * it + c), SC)

            @block.scalar
            def _(act):
                def prep(n, p, slot, u, kind, band):
                    act.wait_ge(x_in[slot], 32 * u + 32)
                    act.wait_ge(tiles, PAIRS * n + PAIRS)
                    v = xs[slot][:, :].rearrange("p (r w) -> p r w", w=W)

                    def part(dst, lanes, r0, r1):
                        return act.activation(dst, v[lanes, r0:r1, :], ACT.Identity, scale=norm_now[lanes, 0:1],
                                              bias=norm_now[lanes, 1:2])
                    up, dn = slice(0, C), slice(C, P)
                    part(same[p][0][up, :, 1:1 + W], up, 0, RH).then_inc(act_prep, 1)
                    part(same[p][1][dn, :, 1:1 + W], dn, 0, RH).then_inc(act_prep, 1)
                    act.wait_ge(dve_prep, n + 1)
                    act.activation(xn[:, :], xs[slot][:, :], ACT.Identity, scale=norm_now[:, 0:1], bias=norm_now[:, 1:2]).then_inc(act_prep, 1)
                    part(next_[p][0][dn, 0:RH - 1, 1:1 + W], up, 1, RH).then_inc(act_prep, 1)
                    part(next_[p][1][up, 0:RH - 1, 1:1 + W], dn, 1, RH).then_inc(act_prep, 1)

                with act.Fori(0, B) as i:
                    act.wait_ge(normed, INNER * i + 1)
                    act.wait_ge(act_prep, 5 * NB * i + 1)
                    act.copy(norm_now[:, :], norm[:, :]).then_inc(norm_taken, 1)
                    act.wait_ge(norm_taken, i + 1)
                    for b in opening(i):
                        prep(*b)
                    with act.Fori(0, INNER) as it:
                        for j in range(TURN):
                            prep(*inner(i, it, j))

            @block.vector
            def _(dve):
                up, dn = slice(0, C), slice(C, P)

                def prep(n, p, kind, i, between=lambda: None):
                    dve.wait_ge(tiles, PAIRS * n + PAIRS)
                    dve.wait_ge(act_prep, 5 * n + 3)
                    dve.tensor_copy(next_[p][0][up, 0:RH - 1, :], same[p][0][up, 0:RH - 1, :])
                    dve.tensor_copy(next_[p][1][dn, 0:RH - 1, :], same[p][1][dn, 0:RH - 1, :])
                    between()
                    dve.wait_ge(act_prep, 5 * n + 4)
                    nv = xn[:, :].rearrange("p (r w) -> p r w", w=W)
                    dve.tensor_tensor(same[p][0][dn, :, 1:1 + W], nv[up, :, :], same[p][0][up, :, 1:1 + W], ALU.subtract)
                    between()
                    last = dve.tensor_tensor(same[p][1][up, :, 1:1 + W], nv[dn, :, :], same[p][1][dn, :, 1:1 + W], ALU.subtract)
                    if kind != IN:
                        last.then_inc(split_edge, 1)
                        dve.wait_ge(act_prep, 5 * n + 6)
                        dve.wait_ge(split_edge, 2 * i + (1 if kind == BOTTOM else 2))
                        if kind == TOP:
                            dve.memset(same[p][0][:, 0, :], 0.0)
                            last = dve.memset(next_[p][0][up, 0, :], 0.0)
                        else:
                            dve.memset(same[p][1][:, RH - 1, :], 0.0)
                            last = dve.memset(next_[p][1][up, RH - 2, :], 0.0)
                    last.then_inc(dve_prep, 1)

                def read_out(n, band, p, between=lambda: None):
                    for q in range(PAIRS):
                        dve.wait_ge(tiles, PAIRS * n + PAIRS + q + 1)
                        dve.wait_ge(added, PAIRS * n + q + 1)
                        dve.scalar_tensor_tensor(stage[:, q, :], psum[PAIRS * p + q][:, 0:NT], w_max[:, 0:1],
                                                 e_map[:, bass.ds((band * R + 2 * q) * W, NT)], ALU.mult, ALU.add)\
                           .then_inc(evac, 1)
                        if q == 1:
                            between()

                def take_stats(m, turn, rec, cols):
                    dve.wait_ge(stat_in[m], 32 * turn + 32)
                    dve.bn_stats(records[:, bass.ds(rec, 1), :].rearrange("p a b -> p (a b)"), sx[m][:, 0:cols])\
                       .then_inc(stat_used, 1)

                for p in range(2):
                    for s in range(2):
                        for buf in (same[p][s], next_[p][s]):
                            last = dve.memset(buf[:, :, :], 0.0)
                    last.then_inc(tiles, PAIRS)
                dve.wait_ge(tiles, 2 * PAIRS)
                dve.memset(newt[:, 0:1], 0.0).then_inc(stat_used, SX)
                for k, counter in enumerate((dve_prep, act_prep, root_ready, evac)):
                    dve.memset(quad[:, k, :], 0.0).then_inc(counter, 1)
                dve.memset(dev2[:, 0:1], 0.0).then_inc(normed, 1)
                dve.wait_ge(stat_used, SX)
                dve.wait_ge(evac, 1)
                with dve.Fori(0, B) as i:
                    before = INNER * TURN
                    for k, (n, p, slot, u, kind, band) in enumerate(opening(i)):
                        left = opening_chunks(k)

                        def chunk():
                            if left:
                                c = left.pop(0)
                                take_stats(c % SX, CPI // SX * i + c // SX, c, OPEN_COLS[c])
                        chunk()
                        prep(n, p, kind, i, chunk)
                        chunk()
                        if k == 1:
                            dve.wait_ge(evac, PAIRS * n + 1)
                        read_out(n, before, 1 - p, chunk)
                        before = band
                    with dve.Fori(0, INNER) as it:
                        for j in range(TURN):
                            n, p, slot, u, kind, band = inner(i, it, j)
                            turn = INNER * i + it
                            if j == SB:
                                dve.wait_ge(stat_used, CPI * i + CPO + CPT * it + CPT + SX)
                            left = list(range(CPB * j, CPB * j + CPB)) if j < SB else []

                            def chunk():
                                if left:
                                    c = left.pop(0)
                                    take_stats(c % SX, CPI // SX * i + CPO // SX + CPT // SX * it + c // SX, CPO + CPT * it + c, SC)
                            chunk()
                            prep(n, p, kind, i, chunk)
                            chunk()
                            if j == SB:
                                dve.bn_aggr(mv[:, :], records[:, 0:NSTAT, :].rearrange("p a b -> p (a b)")).then_inc(aggregated, 1)
                            if j == SB + 1:
                                dve.wait_ge(root_ready, turn + 2)
                                dve.wait_ge(norm_taken, i + 1)
                                commit(dve, commits, 5 * turn)
                                dve.tensor_copy(gsum[:, 0:1], norm[:, 0:1]).then_inc(normed, 1)
                            read_out(n, band - 1, 1 - p, chunk)
                            chunk()
                            if j == SB:
                                dve.wait_ge(partners_done, turn + 1)
                                dve.wait_ge(root_ready, turn + 1)
                                combine(dve, chain, 8 * turn, psum[3][:, NT:NT + 6].rearrange("p (a b) -> p a b", a=3))
                                dve.tensor_scalar(gvar[:, :], gsum[:, 1:2], 0.25, EPS, ALU.mult, ALU.add).then_inc(var_ready, 1)
                read_out(NB * B, INNER * TURN, 1)

            @block.tensor
            def _(pe):
                def conv(n, p, last_tile_waits=None):
                    pe.wait_ge(act_prep, 5 * n + 6)
                    pe.wait_ge(dve_prep, n + 2)
                    pe.wait_ge(evac, PAIRS * n + 1)
                    for q in range(PAIRS):
                        if q == PAIRS - 1 and last_tile_waits is not None:
                            pe.wait_ge(*last_tile_waits)
                        o = psum[PAIRS * p + q]
                        y = 2 * q
                        for k in range(15):
                            for s in range(2):
                                if k < 9:
                                    ky, kx = k // 3, k % 3
                                    w, v, r = w_hi[:, k, :], same[p][s], y + ky
                                else:
                                    kx = (k - 9) % 3
                                    w, v, r = w_lo[s][:, k - 9, :], next_[p][s], y + (k >= 12)
                                mm = pe.matmul(o[C * s:C * s + C, 0:NT], w, v[:, r:r + 2, kx:kx + W],
                                               start=(k == 0), stop=(k == 14))
                        mm.then_inc(tiles, 1)

                with pe.Fori(0, B) as i:
                    for b in opening(i):
                        conv(*b[:2])
                    with pe.Fori(0, INNER) as it:
                        for j in range(TURN):
                            n, p = inner(i, it, j)[:2]
                            turn = INNER * i + it
                            if j == SB:
                                pe.wait_ge(evac, PAIRS * n + 1)
                                pe.wait_ge(aggregated, turn + 1)
                                for k in range(3):
                                    mm = pe.matmul(psum[3][:, NT + 2 * k:NT + 2 * k + 2], partner[:, k, :], mv[:, :],
                                                   start=True, stop=True)
                                mm.then_inc(partners_done, 1)
                            conv(n, p, (var_ready, turn + 1) if j == SB else None)

            @block.gpsimd
            def _(pool):
                def finish(i, n, p, slot, u, kind, band):
                    v = xs[slot][:, W:(R + 1) * W]
                    for q in range(PAIRS):
                        pool.wait_ge(evac, PAIRS * n + PAIRS + q + 2)
                        pool.tensor_tensor(v[:, q * NT:q * NT + NT], stage[:, q, :], v[:, q * NT:q * NT + NT], ALU.add)\
                            .then_inc(added, 1)
                    pool.wait_ge(added, 3 * PAIRS + PAIRS * n)
                    for s in range(2):
                        dst = out[bass.ds(i, 1), :, bass.ds(HALF * s + R * band, R), :]
                        pool.dma_start(dst.rearrange("a c h w -> (a c) (h w)"), v[C * s:C * s + C, :]).then_inc(x_free[slot], 16)

                for s in range(XS):
                    for h in range(2):
                        pool.dma_start(xs[s][C * h:C * h + C, :], x[0, :, 0:RH, :].rearrange("c h w -> c (h w)"))\
                            .then_inc(x_free[s], 16)
                pool.memset(stage[:, :, :], 0.0).then_inc(added, 2 * PAIRS)
                pool.wait_ge(added, 2 * PAIRS)
                with pool.Fori(0, B) as i:
                    for b in opening(i):
                        finish(i, *b)
                    with pool.Fori(0, INNER) as it:
                        for j in range(TURN):
                            finish(i, *inner(i, it, j))
                            if j == SB - 1:
                                pool.wait_ge(var_ready, INNER * i + it + 1)
                                pool.tensor_tensor(root[:, :], gvar[:, :], mhalf[:, :], ALU.pow).then_inc(root_ready, 1)
                for s in range(XS):
                    pool.wait_ge(x_free[s], 32 * (B * (1 + INNER if s < TURN else 2) + 1))


def kernel(**inputs):
    import concourse.bacc as bacc
    from concourse.bass_utils import run_bass_kernel_spmd

    a = {k.replace("L0_conv_", ""): np.asarray(v) for k, v in inputs.items()}
    r1 = C // 16

    def columns(low, high):
        m = np.zeros((96, 3), np.float32)
        m[:C, 0], m[:, 1], m[:, 2] = low, high[:96], high[96:]
        return m

    enc = a["W_enc"].transpose(1, 2, 3, 0).reshape(4 * C, TAPS * C)
    arrays = dict(
        constants(),
        x=a["x"],
        w_id=a["W_id"].transpose(1, 2, 3, 0).reshape(C, TAPS, C),
        b_id=a["b_id"].reshape(C, 1),
        wd_low=a["W_dl"].T,
        wd_high=a["W_dh"].T.reshape(C, 3, 3 * C),
        bd=columns(a["b_dl"], a["b_dh"]),
        w1_low=a["W1_low"].T,
        w1_high=a["W1_high"].T.reshape(2, 96, 3 * r1).transpose(1, 0, 2),
        w2_low=a["W2_low"].T,
        w2_high=a["W2_high"].T,
        wa_low=a["W_al"],
        wa_high=a["W_ah"].reshape(2, 96, C, 3).transpose(1, 0, 3, 2).reshape(96, 2, 3 * C),
        ba=columns(a["b_al"], a["b_ah"]),
        enc_low=enc[:C],
        enc_high=enc[C:].reshape(2, 96, TAPS * C).transpose(1, 0, 2),
        b_enc=a["b_enc"].reshape(1, C),
    )
    arrays = {f"in_{k}": np.ascontiguousarray(v) for k, v in arrays.items()}
    nc = bacc.Bacc("TRN2", target_bir_lowering=False, num_devices=1)
    tensors = {k[3:]: nc.dram_tensor(k, v.shape, mybir.dt.from_np(v.dtype), kind="ExternalInput").ap()
               for k, v in arrays.items()}
    out = nc.dram_tensor("out", (B, C, H, W), F32, kind="ExternalOutput").ap()
    conv_preact(nc, tensors, out)
    r = run_bass_kernel_spmd(nc, [arrays], core_ids=[0])
    return r.results[0]["out"]
```
